# Optimizing a Trainium2 kernel written in Bass

```python
import numpy as np
import jax
import jax.numpy as jnp

def _softmax(x, axis=-1):
    return jax.nn.softmax(x, axis=axis)

def _gelu(x):
    return jax.nn.gelu(x, approximate=True)

def _silu(x):
    return jax.nn.silu(x)

def _sigmoid(x):
    return jax.nn.sigmoid(x)

def _layernorm(x, axis=-1, eps=1e-05):
    m = jnp.mean(x, axis=axis, keepdims=True)
    v = jnp.var(x, axis=axis, keepdims=True)
    return (x - m) / jnp.sqrt(v + eps)

def _scatter_add(tgt, idx, src, axis=0):
    return tgt.at[idx].add(src)

def _segment_sum(src, seg, n):
    return jax.ops.segment_sum(src, seg, n)
kernel_name = 'mk_macaron_d1_jaxref_r8_98bd3e'

def setup_inputs(seed: int=0):
    np.random.seed(seed)
    _w = jnp.asarray

    def _L0_attn_setup():
        import jax, jax.numpy as jnp
        import numpy as np
        HIDDEN = 512
        N_HEADS = 32
        N_KV = 8
        HEAD_DIM = HIDDEN // N_HEADS
        Q_PER_KV = N_HEADS // N_KV
        SEQ = 256
        ROPE_BASE = 1000000.0
        POS_SCALE = 1.0
        SM_SCALE = 1.0 / HEAD_DIM
        BLOCK = 64
        LOCAL_BLOCKS = 16
        VERT_STRIDE = 8

        def _blocksparse_mask(seq_len):
            nb = seq_len // BLOCK
            qb = np.arange(nb)[:, None]
            kb = np.arange(nb)[None, :]
            bmask = (kb <= qb) & ((qb - kb < LOCAL_BLOCKS) | ((kb + 1) % VERT_STRIDE == 0))
            emask = np.kron(bmask, np.ones((BLOCK, BLOCK), dtype=bool))
            i = np.arange(seq_len)
            emask &= i[:, None] >= i[None, :]
            return jnp.asarray(emask)

        def _rope(x, cos, sin):
            x1, x2 = jnp.split(x, 2, axis=-1)
            rot = jnp.concatenate([-x2, x1], axis=-1)
            return x * cos[None, :, None, :] + rot * sin[None, :, None, :]
        key = jax.random.key(seed)
        k1, k2, k3, k4, k5 = jax.random.split(key, 5)
        qkv_out = (N_HEADS + 2 * N_KV) * HEAD_DIM
        return {'hidden_states': jax.random.normal(k1, (1, SEQ, HIDDEN), dtype=jnp.float32), 'w_qkv': jax.random.normal(k2, (qkv_out, HIDDEN), dtype=jnp.float32) * 0.02, 'b_qkv': jnp.zeros((qkv_out,), dtype=jnp.float32), 'w_dense': jax.random.normal(k3, (HIDDEN, HIDDEN), dtype=jnp.float32) * 0.02, 'b_dense': jnp.zeros((HIDDEN,), dtype=jnp.float32)}
    _L0_attn_in = _L0_attn_setup()

    def _L0_ffn_setup():
        import jax, jax.numpy as jnp
        import numpy as np
        HID, INTER = (512, 1792)
        B, S = (2, 256)

        def _binary_diff_weight(w, base):
            d = w - base
            coeff = jnp.mean(jnp.abs(d))
            return base + coeff * jnp.sign(d)
        key = jax.random.key(seed)
        ks = jax.random.split(key, 7)
        return {'hidden_states': jax.random.normal(ks[0], (B, S, HID), dtype=jnp.float32), 'w1': jax.random.normal(ks[1], (INTER, HID), dtype=jnp.float32) * 0.02, 'mean_w1': jax.random.normal(ks[2], (INTER, HID), dtype=jnp.float32) * 0.02, 'w2': jax.random.normal(ks[3], (HID, INTER), dtype=jnp.float32) * 0.02, 'mean_w2': jax.random.normal(ks[4], (HID, INTER), dtype=jnp.float32) * 0.02, 'w3': jax.random.normal(ks[5], (INTER, HID), dtype=jnp.float32) * 0.02, 'mean_w3': jax.random.normal(ks[6], (INTER, HID), dtype=jnp.float32) * 0.02}
    _L0_ffn_in = _L0_ffn_setup()
    _d = {'L0_attn_hidden_states': _L0_attn_in['hidden_states'], 'L0_attn_w_qkv': _L0_attn_in['w_qkv'], 'L0_attn_b_qkv': _L0_attn_in['b_qkv'], 'L0_attn_w_dense': _L0_attn_in['w_dense'], 'L0_attn_b_dense': _L0_attn_in['b_dense'], 'L0_ffn_w1': _L0_ffn_in['w1'], 'L0_ffn_mean_w1': _L0_ffn_in['mean_w1'], 'L0_ffn_w2': _L0_ffn_in['w2'], 'L0_ffn_mean_w2': _L0_ffn_in['mean_w2'], 'L0_ffn_w3': _L0_ffn_in['w3'], 'L0_ffn_mean_w3': _L0_ffn_in['mean_w3']}
    _x0 = _d['L0_attn_hidden_states']
    _d['L0_attn_hidden_states'] = jax.random.normal(jax.random.fold_in(jax.random.key(seed), 1), (2, 1024, 512), dtype=_x0.dtype)
    del _x0
    return _d

def reference(L0_attn_hidden_states, L0_attn_w_qkv, L0_attn_b_qkv, L0_attn_w_dense, L0_attn_b_dense, L0_ffn_w1, L0_ffn_mean_w1, L0_ffn_w2, L0_ffn_mean_w2, L0_ffn_w3, L0_ffn_mean_w3):

    def _L0_attn_ref(hidden_states, w_qkv, b_qkv, w_dense, b_dense):
        import jax, jax.numpy as jnp
        import numpy as np
        HIDDEN = 512
        N_HEADS = 32
        N_KV = 8
        HEAD_DIM = HIDDEN // N_HEADS
        Q_PER_KV = N_HEADS // N_KV
        SEQ = 256
        ROPE_BASE = 1000000.0
        POS_SCALE = 1.0
        SM_SCALE = 1.0 / HEAD_DIM
        BLOCK = 64
        LOCAL_BLOCKS = 16
        VERT_STRIDE = 8

        def _blocksparse_mask(seq_len):
            nb = seq_len // BLOCK
            qb = np.arange(nb)[:, None]
            kb = np.arange(nb)[None, :]
            bmask = (kb <= qb) & ((qb - kb < LOCAL_BLOCKS) | ((kb + 1) % VERT_STRIDE == 0))
            emask = np.kron(bmask, np.ones((BLOCK, BLOCK), dtype=bool))
            i = np.arange(seq_len)
            emask &= i[:, None] >= i[None, :]
            return jnp.asarray(emask)

        def _rope(x, cos, sin):
            x1, x2 = jnp.split(x, 2, axis=-1)
            rot = jnp.concatenate([-x2, x1], axis=-1)
            return x * cos[None, :, None, :] + rot * sin[None, :, None, :]
        B, S, _ = hidden_states.shape
        qkv = jnp.einsum('bsh,oh->bso', hidden_states, w_qkv) + b_qkv
        qkv = qkv.reshape(B, S, N_KV, Q_PER_KV + 2, HEAD_DIM)
        q = qkv[:, :, :, :Q_PER_KV].reshape(B, S, N_HEADS, HEAD_DIM)
        k = qkv[:, :, :, Q_PER_KV]
        v = qkv[:, :, :, Q_PER_KV + 1]
        inv_freq = 1.0 / ROPE_BASE ** (jnp.arange(0, HEAD_DIM, 2, dtype=jnp.float32) / HEAD_DIM)
        t = jnp.arange(S, dtype=jnp.float32) * POS_SCALE
        freqs = jnp.outer(t, inv_freq)
        emb = jnp.concatenate([freqs, freqs], axis=-1)
        cos, sin = (jnp.cos(emb), jnp.sin(emb))
        q = _rope(q, cos, sin)
        k = _rope(k, cos, sin)
        k = jnp.repeat(k, Q_PER_KV, axis=2)
        v = jnp.repeat(v, Q_PER_KV, axis=2)
        mask = _blocksparse_mask(S)
        scores = jnp.einsum('bqhd,bkhd->bhqk', q, k) * SM_SCALE
        scores = jnp.where(mask[None, None], scores, jnp.finfo(scores.dtype).min)
        probs = jax.nn.softmax(scores, axis=-1)
        ctx = jnp.einsum('bhqk,bkhd->bqhd', probs, v).reshape(B, S, HIDDEN)
        out = jnp.einsum('bsh,oh->bso', ctx, w_dense) + b_dense
        return out

    def _L0_ffn_ref(hidden_states, w1, mean_w1, w2, mean_w2, w3, mean_w3):
        import jax, jax.numpy as jnp
        import numpy as np
        HID, INTER = (512, 1792)
        B, S = (2, 256)

        def _binary_diff_weight(w, base):
            d = w - base
            coeff = jnp.mean(jnp.abs(d))
            return base + coeff * jnp.sign(d)
        W1 = _binary_diff_weight(w1, mean_w1)
        W2 = _binary_diff_weight(w2, mean_w2)
        W3 = _binary_diff_weight(w3, mean_w3)
        gate = jnp.einsum('bsh,ih->bsi', hidden_states, W1)
        up = jnp.einsum('bsh,ih->bsi', hidden_states, W3)
        h = jax.nn.silu(gate) * up
        return jnp.einsum('bsi,hi->bsh', h, W2)
    x = L0_attn_hidden_states
    x = x + 0.5 * _L0_ffn_ref(_layernorm(x, axis=-1), L0_ffn_w1, L0_ffn_mean_w1, L0_ffn_w2, L0_ffn_mean_w2, L0_ffn_w3, L0_ffn_mean_w3)
    x = x + _L0_attn_ref(_layernorm(x, axis=-1), L0_attn_w_qkv, L0_attn_b_qkv, L0_attn_w_dense, L0_attn_b_dense)
    x = x + 0.5 * _L0_ffn_ref(_layernorm(x, axis=-1), L0_ffn_w1, L0_ffn_mean_w1, L0_ffn_w2, L0_ffn_mean_w2, L0_ffn_w3, L0_ffn_mean_w3)
    return x

_drawn_inputs = setup_inputs


def setup_inputs(seed=0):
    import zlib

    import numpy as np

    out = dict(_drawn_inputs(seed))
    spreads = {'L0_attn_b_qkv': (0.0, 0.1), 'L0_attn_b_dense': (0.0, 0.1)}
    factors = {'L0_attn_w_qkv': 3.231}
    for name, (base, spread) in spreads.items():
        noise = np.random.default_rng([zlib.crc32(name.encode()), seed]).standard_normal(out[name].shape)
        drawn = base * np.exp(spread * noise) if base else spread * noise
        out[name] = jnp.asarray(drawn.astype(out[name].dtype))
    for name, factor in factors.items():
        out[name] = (out[name] * factor).astype(out[name].dtype)
    return out
```

```python
import numpy as np

import concourse.bass as bass
from concourse import mybir

F32 = mybir.dt.float32
F16 = mybir.dt.float16
BF16 = mybir.dt.bfloat16
I32 = mybir.dt.int32
I8 = mybir.dt.int8
ALU = mybir.AluOpType
ACT = mybir.ActivationFunctionType
AX = mybir.AxisListType

P = 128
BATCH, SEQ, HID, INTER = 2, 1024, 512, 1792
HEAD, KV_HEADS, Q_PER_KV = 16, 8, 4
TOKEN_TILES = BATCH * SEQ // P
SEQ_TILES = SEQ // P
HB = HID // P
IT = INTER // P
CHUNK = 512
TPC = CHUNK // P
CHUNKS = TOKEN_TILES // TPC
GROUPS = BATCH * KV_HEADS
PAIRS = GROUPS // 2
SEQ_PAIRS = KV_HEADS // 2
QW = Q_PER_KV * HEAD
QK = 2 * (QW + HEAD)
GW = QK + 2 * HEAD
QKV = SEQ_PAIRS * GW
ROWS = 6 * HEAD
MROWS = ROWS + 3
SM_SCALE = 1.0 / HEAD
EPS = 1e-5
XS = 1024.0
H_BOUND = 2.0 ** 33
NEG = -3.0e38
RSQRT_SEED = 0x5F3759DF
BUF = 4
PBUF = 3

UNITS = [(0, kt) for kt in (0, 1, 2, 3)] + [(1, kt) for kt in (0, 4, 5, 6, 7, 1, 2, 3)]
NU = len(UNITS)
DIAGONAL = [u for u, (c, kt) in enumerate(UNITS) if kt >= 4 * c]
ND = len(DIAGONAL)


NSPLIT = 12


def score_pieces():
    out = []
    for qt in reversed(range(SEQ_TILES)):
        width = P * (qt + 1)
        for k0 in range(0, width, 512):
            w = min(512, width - k0)
            nh = max(1, min(Q_PER_KV, 512 // w))
            out += [(qt, k0, w, list(range(h, h + nh))) for h in range(0, Q_PER_KV, nh)]
    return out


PIECES = score_pieces()
NP_ = len(PIECES)
LEAD = 8
TAIL_AT, ROWMAX_AT = 3, 4


def piece_slots():
    cols = [512 * (c + 1) - max(512 * c, P * kt) for c, kt in UNITS]
    total, at, out = float(sum(cols)), 0.0, []
    done = LEAD
    for n in cols:
        at += n
        upto = LEAD + int(round((NP_ - LEAD) * at / total))
        out.append(list(range(done, upto)))
        done = upto
    return out


SLOTS = piece_slots()
SHARED = {1: ("qk", 0), 2: ("ctx", 1), 3: ("qk", 1), 5: ("qk", 2), 6: ("ctx", 0), 7: ("qk", 3), 9: ("qk", 4)}
ORDER = ["rowmax", ("qk", 0), ("ctx", 1), ("qk", 1), ("qk", 2), ("ctx", 0), ("qk", 3), ("qk", 4)]
QK_ON_DVE = (0,)
QK_ON_ACT = (1, 2, 3, 4)


def num(k):
    i, c = k
    return c if i is None else i * BUF + c


def shift(k, by):
    return k[0], k[1] + by


def buf(k):
    return k[1] % BUF


def pair_of(k):
    i, c = k
    return (c // 2 if i is None else i * (BUF // 2) + c // 2), c % 2


def never(k, least=0):
    return k[0] is None and k[1] < least


def unit_cols(u):
    c, kt = UNITS[u]
    q0 = max(512 * c, P * kt)
    return q0, 512 * (c + 1), q0 - 512 * c


def build(nc, x_in, w1t, m1t, w3t, m3t, w2t, m2t, wqkvt, b_qkv, wdt, b_d, cos_in, sin_in, out):
    from contextlib import ExitStack
    RADD, RMAX = bass.bass_isa.ReduceOp.add, bass.bass_isa.ReduceOp.max

    ctx = ExitStack()
    base = 16512

    def at(name, shape, dt, offset):
        return nc.alloc_sbuf_tensor_at(name, shape, dt, offset=base + offset)

    W_T = HB * INTER * 2
    A0 = 0
    w_all = at("w_all", [P, 3 * W_T], F16, A0)

    def halves(t, at_, a):
        return [t[:, at_ // 2 + i * W_T // 2:at_ // 2 + (i + 1) * W_T // 2].rearrange("p (a b) -> p a b", a=a)
                for i in range(2)]

    w1s, w3s, w2s = halves(w_all, 0, HB), halves(w_all, 2 * W_T, HB), halves(w_all, 4 * W_T, IT)
    X0 = 6 * W_T
    x = at("x", [P, TOKEN_TILES, HID], F32, X0)
    B0 = X0 + TOKEN_TILES * HID * 4
    SLOT = HB * INTER * 5
    wbase = [at(f"wbase{i}", [P, HB * INTER], F32, B0 + i * SLOT) for i in range(2)]
    wsign = [at(f"wsign{i}", [P, HB * INTER], I8, B0 + i * SLOT + HB * INTER * 4) for i in range(2)]
    C0 = B0 + SLOT
    D0 = C0 + SLOT
    stage13 = [at(f"stage13_{i}", [P, INTER], F32, A0 + 4 * W_T + i * INTER * 4) for i in range(2)]
    stage2 = [at(f"stage2_{i}", [P, 2 * HID], F32, C0 + 20480 + i * 2 * HID * 4) for i in range(2)]

    def working(tag, offset):
        return {
            "silu": [at(f"silu{tag}{i}", [P, CHUNK], F32, offset + i * 2048) for i in range(2)],
            "h": [at(f"h{tag}{i}", [P, CHUNK], F32, offset + 4096 + i * 2048) for i in range(2)],
            "hs": [[at(f"h{n}{tag}{i}", [P, CHUNK], F16, offset + 8192 + (2 * i + j) * 1024)
                    for j, n in enumerate(("hi", "lo"))] for i in range(2)],
        }

    ffn1 = working("a", C0 + 8192)
    xt0 = [at("xt0_hi", [P, HB, CHUNK], F16, D0), at("xt0_lo", [P, HB, CHUNK], F16, D0 + 4096)]
    xt1 = [at("xt1_hi", [P, HB, CHUNK], F16, C0), at("xt1_lo", [P, HB, CHUNK], F16, C0 + 4096)]
    xnorm = [at(f"xnorm{i}", [P, HID], F32, D0 + 8192 + i * 2048) for i in range(TPC)]
    K0 = D0 + 16384
    ident = at("ident", [P, P], F32, K0)
    ident16 = at("ident16", [P, P], BF16, K0 + 512)
    negmask = at("negmask", [P, P], BF16, K0 + 768)
    cos = at("cos", [P, SEQ_TILES, HEAD], F32, K0 + 1024)
    sin = at("sin", [P, SEQ_TILES, HEAD], F32, K0 + 1536)
    stats = at("stats", [P, TPC, 6], F32, K0 + 2048)
    mean_var = at("mean_var", [P, TPC, 2], F32, K0 + 2144)
    nw = at("nw", [P, 4, TPC], F32, K0 + 2176)
    dabs = at("dabs", [P, 16], F32, K0 + 2240)
    bmax = at("bmax", [P, 16], F32, K0 + 2304)
    part = at("part", [P, 4, 2], F32, K0 + 2368)
    allr = at("allr", [P, 4, 2], F32, K0 + 2400)
    wc = at("wc", [P, 4, 6], F32, K0 + 2432)
    scal = at("scal", [P, 8], F32, K0 + 2528)
    rec = at("rec", [P, 4, Q_PER_KV], F32, K0 + 2560)
    rowmax = at("rowmax", [P, SEQ_TILES, Q_PER_KV], F32, K0 + 2624)
    rowmax2 = at("rowmax2", [P, SEQ_TILES // 2, Q_PER_KV], F32, K0 + 2752)
    rest = at("rest", [P, SEQ_TILES, Q_PER_KV], F32, K0 + 2816)
    nm = at("nm", [P, SEQ_TILES, 3, Q_PER_KV], BF16, K0 + 2944)
    assert base + K0 + 3136 + 192 <= 229368

    wq = [at("wq_hi", [P, HB, QKV], F16, B0), at("wq_lo", [P, HB, QKV], F16, B0 + 6144)]
    wq_raw = at("wq_raw", [P, HB * QKV], F32, B0 + 12288)
    R0 = C0 + 20480
    qkv_raw = [at(f"qkv_raw{i}", [P, SEQ_PAIRS, GW], F32, R0 + i * 3072) for i in range(2)]
    rot_c = at("rot_c", [P, SEQ_PAIRS, QK], F32, R0 + 6144)
    rot_s = at("rot_s", [P, SEQ_PAIRS, QK], F32, R0 + 8704)
    bq = at("bq", [P, QKV], F32, R0 + 11264)
    store = at("store", [P, PAIRS * SEQ_TILES, GW], F32, 0)
    S1 = PAIRS * SEQ_TILES * GW * 4
    qa = [at(f"qa{i}", [P, Q_PER_KV, SEQ], BF16, S1 + i * 8192) for i in range(BUF)]
    ctx_sb = at("ctx_sb", [P, 512], F32, S1 + BUF * 8192)
    assert S1 + BUF * 8192 + 2048 <= X0
    probs = [at(f"probs{i}", [P, Q_PER_KV, 512], F32, B0 + i * 8192) for i in range(PBUF)]
    E0 = B0 + PBUF * 8192
    parts_q = [at(f"parts_q{i}", [P, SEQ_TILES * Q_PER_KV, ROWS], BF16, E0 + i * 7680) for i in range(2)]
    parts_k = [at(f"parts_k{i}", [P, SEQ_TILES, ROWS], BF16, E0 + i * 7680 + 6144) for i in range(2)]
    left = at("left", [P, SEQ_TILES, QW + HEAD], F32, E0 + 15360)
    mrow = at("mrow", [3 * Q_PER_KV, SEQ], BF16, E0 + 15360 + 2560)
    ka = [at(f"ka{i}", [P, SEQ], BF16, E0 + 15360 + 4608 + i * 2048) for i in range(BUF)]
    vs = [at(f"vs{i}", [P, SEQ_TILES, 32], F32, E0 + 15360 + 4608 + BUF * 2048 + i * 1024) for i in range(BUF)]
    assert E0 + 15360 + 4608 + BUF * 3072 <= B0 + 57344
    wd = at("wd", [P, HB, HID], F32, B0 + 57344)
    bd = at("bd", [P, HID], F32, B0 + 57344 + 8192)
    ctx_t = [at(f"ctx_t{i}", [P, HB, P], F32, B0 + 57344 + 10240 + i * 2048) for i in range(2)]
    assert B0 + 57344 + 14336 == D0
    w2b_all = at("w2b_all", [P, W_T], F16, S1)
    w13b_all = at("w13b_all", [P, 2 * W_T], F16, B0)
    w1b, w3b, w2b = halves(w13b_all, 0, HB), halves(w13b_all, 2 * W_T, HB), halves(w2b_all, 0, IT)
    ffn2 = working("b", 8192)
    xt1b = [at("xt1b_hi", [P, HB, CHUNK], F16, 0), at("xt1b_lo", [P, HB, CHUNK], F16, 4096)]

    ps = ctx.enter_context(nc.psum_tensor("ps", [P, 8, 512], F32))
    GATE, UP, DOWN, LNT = 0, 1, 2, 6
    CTX_BANK, PASS1, SHARED_BANK = 4, 5, 7

    spill = nc.dram_tensor("spill", [P, 6 * W_T // 2], F16)

    def sem(name):
        return ctx.enter_context(nc.semaphore(name))

    x_loaded = [sem(f"x_loaded{i}") for i in range(CHUNKS)]
    w_loaded = [sem(f"w_loaded{i}") for i in range(2)]
    tables_loaded, wq_loaded, wd_loaded = sem("tables_loaded"), sem("wq_loaded"), sem("wd_loaded")
    spilled, w2_back, w13_back = sem("spilled"), sem("w2_back"), sem("w13_back")
    consts_ready = sem("consts_ready")
    ones_ready = sem("ones_ready")
    diff_ready = sem("diff_ready")
    sign_ready = sem("sign_ready")
    bmax_ready = sem("bmax_ready")
    part_ready = sem("part_ready")
    allr_ready = sem("allr_ready")
    weff_ready = sem("weff_ready")
    whi_ready, wlo_ready = sem("whi_ready"), sem("wlo_ready")
    dve_chain = sem("dve_chain")
    pool_chain = sem("pool_chain")
    xnorm_ready = sem("xnorm_ready")
    lnt_full = sem("lnt_full")
    xhi_ready, xlo_ready = sem("xhi_ready"), sem("xlo_ready")
    gate_full, up_full, down_full = sem("gate_full"), sem("up_full"), sem("down_full")
    silu_ready, h_ready = sem("silu_ready"), sem("h_ready")
    hhi_ready, hlo_ready = sem("hhi_ready"), sem("hlo_ready")
    resid_ready = sem("resid_ready")
    out_stored = sem("out_stored")
    qkv_full, raw_ready = sem("qkv_full"), sem("raw_ready")
    rot_ready, qk_ready, v_ready = sem("rot_ready"), sem("qk_ready"), sem("v_ready")
    split_step = sem("split_step")
    pool_waited, vs_ready = sem("pool_waited"), sem("vs_ready")
    qkt_full = sem("qkt_full")
    qkt_dve, qkt_act = sem("qkt_dve"), sem("qkt_act")
    p1_full, p1_read = sem("p1_full"), sem("p1_read")
    max_step = sem("max_step")
    nm_ready, mt_full, mrow_ready, m_placed = sem("nm_ready"), sem("mt_full"), sem("mrow_ready"), sem("m_placed")
    st_full, exp_ready, diag_ready, pv_full = sem("st_full"), sem("exp_ready"), sem("diag_ready"), sem("pv_full")
    ctx_ready, ctxt_full, rec_ready, norm_ready = sem("ctx_ready"), sem("ctxt_full"), sem("rec_ready"), sem("norm_ready")
    dt_full, ctx_t_ready, dense_full, bias_ready, x2_ready = (
        sem("dt_full"), sem("ctx_t_ready"), sem("dense_full"), sem("bias_ready"), sem("x2_ready"))

    block = ctx.enter_context(nc.Block())

    PIECE13, PIECE2 = INTER, 2 * HID
    WEIGHTS = [(w1s, 0, 0, 4, PIECE13), (w3s, 1, 4, 4, PIECE13), (w2s, 0, 8, 7, PIECE2)]

    def staged(w, p):
        return (stage2 if w == 2 else stage13)[p % 2]

    def loads_of(piece):
        return w_loaded[piece % 2], 32 * (piece // 2 + 1)

    def half(w, j, p):
        cols = WEIGHTS[w][4]
        t = WEIGHTS[w][0][j]
        return t.rearrange("p a b -> p (a b)")[:, p * cols:(p + 1) * cols]

    def x_tiles_ready(eng, n):
        if n < 4:
            eng.wait_ge(x_loaded[n], 16)
        elif n < 8:
            eng.wait_ge(resid_ready, TPC * (n - 4) + TPC)
        else:
            eng.wait_ge(x2_ready, TPC * (n - 8) + TPC)

    def xt_of(n):
        return xt0 if n % 2 == 0 else (xt1b if n >= 8 else xt1)

    @block.sync
    def _(sp):
        x_rows = x_in.rearrange("(n p) h -> p n h", p=P)
        out_rows = out.rearrange("(n p) h -> p n h", p=P)

        def load_x(c):
            sp.dma_start(x[:, TPC * c:TPC * (c + 1), :], x_rows[:, TPC * c:TPC * (c + 1), :]).then_inc(x_loaded[c], 16)

        load_x(0)
        sources = [(w1t, m1t), (w3t, m3t), (w2t, m2t)]
        for w, (_, slot, first, n, cols) in enumerate(WEIGHTS):
            for p in range(n):
                piece = first + p
                if piece >= 2:
                    sp.wait_ge(sign_ready, 2 * (piece - 1))
                if w == 2 and p == 0:
                    sp.wait_ge(wlo_ready, 8)
                view = [s.rearrange("(t p) n -> p t n", p=P) for s in sources[w]]
                per = cols // view[0].shape[2]
                src = [v[:, per * p:per * (p + 1), :] for v in view]
                sp.dma_start(wbase[slot][:, p * cols:(p + 1) * cols].rearrange("p (t n) -> p t n", t=per), src[1])\
                    .then_inc(w_loaded[piece % 2], 16)
                sp.dma_start(staged(w, p)[:, :].rearrange("p (t n) -> p t n", t=per), src[0])\
                    .then_inc(w_loaded[piece % 2], 16)
            if w == 1:
                for c in range(1, CHUNKS):
                    load_x(c)
        cs = [t.rearrange("(n p) d -> p n d", p=P) for t in (cos_in, sin_in)]
        sp.dma_start(cos[:, :, :], cs[0]).then_inc(tables_loaded, 16)
        sp.dma_start(sin[:, :, :], cs[1]).then_inc(tables_loaded, 16)
        sp.wait_ge(whi_ready, 15)
        sp.wait_ge(wlo_ready, 15)
        sp.dma_start(spill.ap(), w_all[:, :]).then_inc(spilled, 16)
        sp.dma_start(wq_raw[:, :].rearrange("p (t n) -> p t n", t=HB), wqkvt.rearrange("(t p) n -> p t n", p=P))\
            .then_inc(wq_loaded, 16)
        sp.dma_start(bq[:, :], b_qkv.partition_broadcast(P)).then_inc(tables_loaded, 16)
        sp.wait_ge(qk_ready, TOKEN_TILES)
        sp.wait_ge(raw_ready, 2 * TOKEN_TILES)
        sp.wait_ge(v_ready, TOKEN_TILES)
        sp.dma_start(wd[:, :, :], wdt.rearrange("(t p) n -> p t n", p=P)).then_inc(wd_loaded, 16)
        sp.dma_start(bd[:, :], b_d.partition_broadcast(P)).then_inc(wd_loaded, 16)

        def place_rowmax(g):
            sp.wait_ge(mrow_ready, num(g) + 1)
            for i in range(3):
                sp.dma_start(qa[buf(g)][ROWS + i:ROWS + i + 1, :, :], mrow[4 * i:4 * i + 4, :])\
                    .then_inc(m_placed, 16)

        with sp.Fori(0, GROUPS // BUF) as i:
            for u in range(BUF):
                place_rowmax((i, u))
        sp.wait_ge(pv_full, NU * GROUPS)
        sp.wait_ge(norm_ready, 2 * GROUPS)
        sp.wait_ge(spilled, 16)
        sp.dma_start(w13b_all[:, :], spill.ap()[:, 0:2 * W_T]).then_inc(w13_back, 16)
        sp.dma_start(w2b_all[:, :], spill.ap()[:, 2 * W_T:3 * W_T]).then_inc(w2_back, 16)
        for c in range(CHUNKS):
            sp.wait_ge(resid_ready, TOKEN_TILES + TPC * (c + 1))
            sp.dma_start(out_rows[:, TPC * c:TPC * (c + 1), :], x[:, TPC * c:TPC * (c + 1), :]).then_inc(out_stored, 16)
        sp.wait_ge(out_stored, 16 * CHUNKS)

    @block.gpsimd
    def _(pool):
        steps = [0]

        def chain(ins):
            steps[0] += 1
            ins.then_inc(pool_chain, 1)
            pool.wait_ge(pool_chain, steps[0])

        chain(nc.gpsimd.memset(ident[:, :], 0.0))
        chain(nc.gpsimd.memset(ident16[:, :], 0.0))
        chain(nc.gpsimd.memset(negmask[:, :], 0.0))
        for m in (ident, ident16):
            nc.gpsimd.affine_select(out=m[:, :], in_=m[:, :], compare_op=ALU.not_equal, fill=1.0, base=0,
                                    pattern=[[-1, P]], channel_multiplier=1).then_inc(consts_ready, 1)
        nc.gpsimd.affine_select(out=negmask[:, :], in_=negmask[:, :], compare_op=ALU.is_ge, fill=NEG, base=0,
                                pattern=[[-1, P]], channel_multiplier=1).then_inc(consts_ready, 1)

        def differences(w):
            _, slot, first, n, cols = WEIGHTS[w]
            for p in range(n):
                pool.wait_ge(*loads_of(first + p))
                st = staged(w, p)[:, :]
                nc.gpsimd.tensor_tensor(out=st, in0=st, in1=wbase[slot][:, p * cols:(p + 1) * cols],
                                        op=ALU.subtract).then_inc(diff_ready, 1)

        def over_partitions(w):
            pool.wait_ge(part_ready, w + 1)
            nc.gpsimd.partition_all_reduce(allr[:, w, 0:1], part[:, w, 0:1], P, RADD).then_inc(allr_ready, 1)
            nc.gpsimd.partition_all_reduce(allr[:, w, 1:2], part[:, w, 1:2], P, RMAX).then_inc(allr_ready, 1)

        for w in range(3):
            differences(w)
            over_partitions(w)
        over_partitions(3)

        raw4 = [r[:, :, 0:QK].rearrange("p g (h d) -> p g h d", d=HEAD) for r in qkv_raw]
        c4, s4 = (t[:, :, :].rearrange("p g (h d) -> p g h d", d=HEAD) for t in (rot_c, rot_s))
        H2 = HEAD // 2
        pool.wait_ge(tables_loaded, 48)
        for i in range(TOKEN_TILES):
            r, tt = raw4[i % 2], i % SEQ_TILES
            pool.wait_ge(raw_ready, 2 * (i + 1))
            if i:
                pool.wait_ge(qk_ready, i)

            def table(t, lo, hi):
                return t[:, tt, lo:hi].unsqueeze(1).unsqueeze(1).to_broadcast([P, SEQ_PAIRS, QK // HEAD, hi - lo])

            nc.gpsimd.tensor_tensor(out=c4, in0=r, in1=table(cos, 0, HEAD), op=ALU.mult).then_inc(rot_ready, 1)
            for lo in (0, H2):
                nc.gpsimd.tensor_tensor(out=s4[:, :, :, lo:lo + H2], in0=r[:, :, :, H2 - lo:HEAD - lo],
                                        in1=table(sin, lo, lo + H2), op=ALU.mult).then_inc(rot_ready, 1)

        def wait(semaphore, value):
            pool.wait_ge(semaphore, value)
            if not isinstance(value, int):
                pool.sem_inc(pool_waited, 1)


        def split_steps(g):
            pair, odd = pair_of(g)
            rows = store[:, bass.ds(pair * SEQ_TILES, SEQ_TILES), :]
            q_in = rows[:, :, QW * odd:QW * (odd + 1)].rearrange("p t (h d) -> p t h d", d=HEAD)
            k_in = rows[:, :, 2 * QW + HEAD * odd:2 * QW + HEAD * (odd + 1)]
            q2, kk = parts_q[g[1] % 2], parts_k[g[1] % 2]
            qs = q2[:, :, :].rearrange("p (t h) r -> p t h r", h=Q_PER_KV)
            lq = left[:, :, 0:QW].rearrange("p t (h d) -> p t h d", d=HEAD)
            lk = left[:, :, QW:QW + HEAD]

            def slot(t, s, n=1):
                return t[:, :, HEAD * s:HEAD * (s + n)]

            def slot4(s):
                return qs[:, :, :, HEAD * s:HEAD * (s + 1)]

            copy, sub = nc.gpsimd.tensor_copy, lambda o, a, b: nc.gpsimd.tensor_tensor(out=o, in0=a, in1=b, op=ALU.subtract)
            return [
                lambda: copy(slot4(0), q_in),
                lambda: copy(slot(kk, 0), k_in),
                lambda: sub(lq, q_in, slot4(0)),
                lambda: sub(lk, k_in, slot(kk, 0)),
                lambda: copy(slot4(1), lq),
                lambda: copy(slot(kk, 1), lk),
                lambda: sub(slot4(5), lq, slot4(1)),
                lambda: sub(slot(kk, 4), lk, slot(kk, 1)),
                lambda: copy(q2[:, :, 2 * HEAD:4 * HEAD], q2[:, :, 0:2 * HEAD]),
                lambda: copy(slot(q2, 4), slot(q2, 0)),
                lambda: copy(slot(kk, 2), slot(kk, 1)),
                lambda: copy(kk[:, :, 3 * HEAD:6 * HEAD].rearrange("p t (s d) -> p t s d", d=HEAD)[:, :, 0:3:2, :],
                             kk[:, :, 0:HEAD].unsqueeze(2).to_broadcast([P, SEQ_TILES, 2, HEAD])),
            ]

        def split(g, lo, hi):
            todo = split_steps(g)
            for n in range(lo, hi):
                if n == 0:
                    if not never(g, 2):
                        wait(qkt_full, 5 * (num(g) - 1))
                else:
                    wait(split_step, num(g) * NSPLIT + n)
                todo[n]().then_inc(split_step, 1)

        def copy_v(g):
            pair, odd = pair_of(g)
            if never(g, 1):
                wait(ones_ready, BUF)
            if not never(g, 3):
                wait(pv_full, NU * (num(g) - 2))
            nc.gpsimd.tensor_copy(vs[buf(g)][:, :, 0:HEAD], store[:, bass.ds(pair * SEQ_TILES, SEQ_TILES),
                                                                  QK + HEAD * odd:QK + HEAD * (odd + 1)])\
                .then_inc(vs_ready, 1)

        def mask_unit(g, u):
            d = DIAGONAL.index(u)
            wait(exp_ready, 2 * (num(g) * NU + u) + 2)
            p = probs[u % PBUF][:, :, 0:P]
            nc.gpsimd.affine_select(out=p, in_=p, compare_op=ALU.is_ge, fill=0.0, base=0,
                                    pattern=[[0, Q_PER_KV], [1, P]], channel_multiplier=-1).then_inc(diag_ready, 1)

        def body(k, first, second, ahead):
            if first:
                copy_v(k)
            for s in range(NU):
                if second and s in DIAGONAL:
                    mask_unit(shift(k, -1), s)
                if ahead:
                    split(shift(k, 2), s, s + 1)

        pool.wait_ge(qk_ready, TOKEN_TILES)
        pool.wait_ge(v_ready, TOKEN_TILES)
        split((None, 0), 0, NSPLIT)
        split((None, 1), 0, NSPLIT)
        for k in (0, 1):
            body((None, k), True, k >= 1, True)
        with pool.Fori(0, 3) as i:
            for u in range(BUF):
                body((i, u + 2), True, True, True)
        for k in (14, 15, 16):
            body((None, k), k < GROUPS, True, False)

    @block.scalar
    def _(act):
        def signs(w, p):
            _, slot, first, n, cols = WEIGHTS[w]
            piece = first + p
            act.wait_ge(diff_ready, piece + 1)
            st = staged(w, p)[:, :]
            if p == 0 and w == 2:
                act.wait_ge(weff_ready, 4)
            nc.scalar.activation(wsign[slot][:, p * cols:(p + 1) * cols], st, ACT.Sign).then_inc(sign_ready, 1)
            nc.scalar.activation(st, st, ACT.Abs, accum_out=dabs[:, piece:piece + 1]).then_inc(sign_ready, 1)

        def split_hi(w, p):
            _, slot, first, n, cols = WEIGHTS[w]
            act.wait_ge(weff_ready, first + p + 1)
            nc.scalar.activation(half(w, 0, p), wbase[slot][:, p * cols:(p + 1) * cols], ACT.Copy,
                                 scale=wc[:, w, 3:4]).then_inc(whi_ready, 1)

        def ln_hi(n, j):
            act.wait_ge(lnt_full, TPC * n + j + 1)
            nc.scalar.copy(xt_of(n)[0][:, :, j * P:(j + 1) * P],
                           ps[:, LNT + j % 2, :].rearrange("p (a b) -> p a b", a=HB)).then_inc(xhi_ready, 1)

        for p in range(4):
            signs(0, p)
        for j in range(TPC):
            ln_hi(0, j)
        for p in range(2):
            signs(1, p)
        for p in range(4):
            split_hi(0, p)
            if p < 2:
                signs(1, p + 2)
        for p in range(4):
            split_hi(1, p)
        for p in range(7):
            signs(2, p)

        def silu(T, u, bufs):
            act.wait_ge(gate_full, T + 1)
            if not isinstance(T, int) or T >= 2:
                act.wait_ge(h_ready, T - 1)
            nc.scalar.activation(bufs["silu"][u][:, :], ps[:, GATE, :], ACT.Silu, scale=scal[:, 0:1])\
                .then_inc(silu_ready, 1)

        def h_hi(T, u, bufs):
            act.wait_ge(h_ready, T + 1)
            if not isinstance(T, int) or T >= 2:
                act.wait_ge(down_full, T - 1)
            nc.scalar.copy(bufs["hs"][u][0][:, :], bufs["h"][u][:, :]).then_inc(hhi_ready, 1)

        def ffn(f, bufs):
            for c in range(CHUNKS):
                T0 = f * CHUNKS * IT + c * IT
                ln = (1, 2, 3, 4)[c] if f == 0 else (9, 10, 11, None)[c]
                if f == 0 and c == 0:
                    act.wait_ge(dve_chain, SCAL_READY)
                for t in (0, 1):
                    silu(T0 + t, t % 2, bufs)
                    if f == 0 and c == 0 and t == 0:
                        for p in range(7):
                            split_hi(2, p)
                    h_hi(T0 + t, t % 2, bufs)
                if f == 0 and c == 2:
                    act.wait_ge(dve_chain, WQ_READY)
                    nc.scalar.activation(wq[0][:, :, :].rearrange("p a b -> p (a b)"), wq_raw[:, :], ACT.Copy,
                                         scale=wc[:, 3, 3:4]).then_inc(whi_ready, 1)
                with act.Fori(1, 6) as i:
                    for t in (0, 1):
                        T = i * 2 + (T0 + t)
                        silu(T, t, bufs)
                        h_hi(T, t, bufs)
                for t in (IT - 2, IT - 1):
                    if t == IT - 2 and ln is not None:
                        ln_hi(ln, 0)
                        ln_hi(ln, 1)
                    silu(T0 + t, t % 2, bufs)
                    if t == IT - 2 and ln is not None:
                        ln_hi(ln, 2)
                        ln_hi(ln, 3)
                    h_hi(T0 + t, t % 2, bufs)

        ffn(0, ffn1)

        st4 = store[:, :, :].rearrange("p (g t) c -> p g t c", t=SEQ_TILES)
        for i in range(TOKEN_TILES):
            m, j = divmod(i, TPC)
            b, tt = divmod(i, SEQ_TILES)
            if m < CHUNKS - 1 and j == 2:
                ln_hi(5 + m, 0)
                ln_hi(5 + m, 1)
            if m < CHUNKS - 1 and j == 3:
                ln_hi(5 + m, 2)
                ln_hi(5 + m, 3)
            act.wait_ge(raw_ready, 2 * (i + 1))
            if i == 0:
                act.wait_ge(spilled, 16)
            nc.scalar.copy(st4[:, SEQ_PAIRS * b:SEQ_PAIRS * (b + 1), tt, QK:GW], qkv_raw[i % 2][:, :, QK:GW])\
                .then_inc(v_ready, 1)

        def exps(g, u):
            q0, q1, _ = unit_cols(u)
            U = num(g) * NU + u
            for pair in range(2):
                act.wait_ge(st_full, U * 2 + pair + 1)
                if not (never(g, 1) and u < PBUF):
                    act.wait_ge(pv_full, U - PBUF + 1)
                nc.scalar.activation(probs[u % PBUF][:, 2 * pair:2 * pair + 2, 0:q1 - q0],
                                     ps[:, 2 * pair:2 * pair + 2, 0:q1 - q0], ACT.Exp, scale=SM_SCALE)\
                    .then_inc(exp_ready, 1)

        def take_context(g, c):
            act.wait_ge(pv_full, num(g) * NU + (4 if c == 0 else NU))
            if c or not never(g, 1):
                act.wait_ge(ctxt_full, num(g) * 2 + c)
            nc.scalar.copy(ctx_sb[:, :], ps[:, CTX_BANK, :]).then_inc(ctx_ready, 1)

        def take_qk(g, h):
            act.wait_ge(qkt_full, num(g) * 5 + h + 1)
            dst = ka[buf(g)][0:ROWS, :] if h == 4 else qa[buf(g)][0:ROWS, h, :]
            nc.scalar.copy(dst, ps[0:ROWS, SHARED_BANK, :].bitcast(BF16)).then_inc(qkt_act, 1)

        def body(k, second, ahead, tail):
            for s in range(NU):
                if s == 0 and tail:
                    take_context(shift(k, -2), 1)
                if second:
                    exps(shift(k, -1), s)
                use = SHARED.get(s)
                if use and use[0] == "qk" and use[1] in QK_ON_ACT and ahead:
                    take_qk(shift(k, 1), use[1])
                if s == 4 and second:
                    take_context(shift(k, -1), 0)

        act.wait_ge(ones_ready, BUF)
        for h in QK_ON_ACT:
            take_qk((None, 0), h)
        for k in (0, 1):
            body((None, k), k >= 1, True, False)
        with act.Fori(0, 3) as i:
            for u in range(BUF):
                body((i, u + 2), True, True, True)
        for k in (14, 15, 16):
            body((None, k), True, k + 1 < GROUPS, True)
        take_context((None, GROUPS - 1), 1)

        def take_ctx_t(i):
            act.wait_ge(dt_full, i + 1)
            if i >= 2:
                act.wait_ge(dense_full, i - 1)
            nc.scalar.copy(ctx_t[i % 2][:, :, :].rearrange("p a b -> p (a b)"), ps[:, 4 + i % 2, :])\
                .then_inc(ctx_t_ready, 1)

        for i in range(TOKEN_TILES):
            take_ctx_t(i)
            if i in (12, 13):
                ln_hi(8, 2 * (i - 12))
                ln_hi(8, 2 * (i - 12) + 1)
        ffn(1, ffn2)

    @block.vector
    def _(dve):
        steps = [0]

        def chain(ins):
            steps[0] += 1
            ins.then_inc(dve_chain, 1)
            dve.wait_ge(dve_chain, steps[0])

        def layer_norm(n):
            tiles = [TPC * (n % 4) + j for j in range(TPC)]
            x_tiles_ready(dve, n)
            for j, i in enumerate(tiles):
                chain(nc.vector.bn_stats(out=stats[:, j, :], in_=x[:, i, :]))
            for j in range(TPC):
                chain(nc.vector.bn_aggr(out=mean_var[:, j, :], in_=stats[:, j, :]))
            var, y, a, b = (nw[:, i, :] for i in range(4))
            chain(nc.vector.tensor_scalar(var, mean_var[:, :, 1], EPS, None, ALU.add))
            chain(nc.vector.tensor_scalar(a.bitcast(I32), var.bitcast(I32), 1, None, ALU.logical_shift_right))
            chain(nc.vector.tensor_scalar(y.bitcast(I32), a.bitcast(I32), -1, RSQRT_SEED, ALU.mult, ALU.add))
            for _ in range(3):
                chain(nc.vector.tensor_tensor(out=a, in0=y, in1=y, op=ALU.mult))
                chain(nc.vector.tensor_tensor(out=b, in0=a, in1=var, op=ALU.mult))
                chain(nc.vector.tensor_scalar(a, b, -0.5, 1.5, ALU.mult, ALU.add))
                chain(nc.vector.tensor_tensor(out=y, in0=y, in1=a, op=ALU.mult))
            chain(nc.vector.tensor_scalar(a, y, XS, None, ALU.mult))
            if n:
                dve.wait_ge(lnt_full, TPC * n)
            for j, i in enumerate(tiles):
                nc.vector.tensor_scalar(xnorm[j][:, :], x[:, i, :], mean_var[:, j, 0:1], nw[:, 2, j:j + 1],
                                        ALU.subtract, ALU.mult).then_inc(xnorm_ready, 1)

        def ln_lo(n, j):
            dve.wait_ge(xhi_ready, TPC * n + j + 1)
            nc.vector.tensor_tensor(out=xt_of(n)[1][:, :, j * P:(j + 1) * P],
                                    in0=ps[:, LNT + j % 2, :].rearrange("p (a b) -> p a b", a=HB),
                                    in1=xt_of(n)[0][:, :, j * P:(j + 1) * P], op=ALU.subtract).then_inc(xlo_ready, 1)

        def base_max(w, p):
            _, slot, first, n, cols = WEIGHTS[w]
            dve.wait_ge(*loads_of(first + p))
            nc.vector.tensor_reduce(bmax[:, first + p:first + p + 1], wbase[slot][:, p * cols:(p + 1) * cols],
                                    AX.X, ALU.max, apply_absolute_value=True).then_inc(bmax_ready, 1)

        def power_of_two(w):
            bound, e, s, inv = (wc[:, w, i:i + 1] for i in (1, 2, 3, 4))
            tmp = wc[:, w, 5:6]
            chain(nc.vector.tensor_scalar(bound, bound, 2.0 ** -30, None, ALU.max))
            chain(nc.vector.tensor_scalar(e.bitcast(I32), bound.bitcast(I32), 23, None, ALU.logical_shift_right))
            chain(nc.vector.tensor_scalar(tmp.bitcast(I32), e.bitcast(I32), -1, 268, ALU.mult, ALU.add))
            chain(nc.vector.tensor_scalar(s.bitcast(I32), tmp.bitcast(I32), 23, None, ALU.logical_shift_left))
            chain(nc.vector.tensor_scalar(tmp.bitcast(I32), e.bitcast(I32), -14, None, ALU.add))
            chain(nc.vector.tensor_scalar(inv.bitcast(I32), tmp.bitcast(I32), 23, None, ALU.logical_shift_left))

        def weight_stats(w):
            _, slot, first, n, cols = WEIGHTS[w]
            dve.wait_ge(sign_ready, 2 * (first + n))
            dve.wait_ge(bmax_ready, first + n)
            nc.vector.tensor_reduce(part[:, w, 0:1], dabs[:, first:first + n], AX.X, ALU.add)
            nc.vector.tensor_reduce(part[:, w, 1:2], bmax[:, first:first + n], AX.X, ALU.max).then_inc(part_ready, 1)
            dve.wait_ge(allr_ready, 2 * (w + 1))
            chain(nc.vector.tensor_scalar(wc[:, w, 0:1], allr[:, w, 0:1], 1.0 / (INTER * HID), None, ALU.mult))
            chain(nc.vector.tensor_tensor(out=wc[:, w, 1:2], in0=wc[:, w, 0:1], in1=allr[:, w, 1:2], op=ALU.add))
            power_of_two(w)

        def effective(w, p):
            _, slot, first, n, cols = WEIGHTS[w]
            b = wbase[slot][:, p * cols:(p + 1) * cols]
            nc.vector.scalar_tensor_tensor(out=b, in0=wsign[slot][:, p * cols:(p + 1) * cols], scalar=wc[:, w, 0:1],
                                           in1=b, op0=ALU.mult, op1=ALU.add).then_inc(weff_ready, 1)

        def split_lo(w, p):
            _, slot, first, n, cols = WEIGHTS[w]
            dve.wait_ge(whi_ready, first + p + 1)
            nc.vector.scalar_tensor_tensor(out=half(w, 1, p), in0=wbase[slot][:, p * cols:(p + 1) * cols],
                                           scalar=wc[:, w, 3:4], in1=half(w, 0, p), op0=ALU.mult,
                                           op1=ALU.subtract).then_inc(wlo_ready, 1)

        def finish_weight(w, n):
            for p in range(n + 1):
                if p < n:
                    effective(w, p)
                if p:
                    split_lo(w, p - 1)

        layer_norm(0)
        for p in range(4):
            base_max(0, p)
        for j in range(TPC):
            ln_lo(0, j)
        weight_stats(0)
        finish_weight(0, 4)
        for p in range(4):
            base_max(1, p)
        weight_stats(1)
        finish_weight(1, 4)
        for p in range(7):
            base_max(2, p)
        weight_stats(2)
        chain(nc.vector.tensor_scalar(scal[:, 0:1], wc[:, 0, 4:5], 1.0 / XS, None, ALU.mult))
        chain(nc.vector.tensor_scalar(scal[:, 1:2], wc[:, 0, 3:4], 1.0 / (XS * H_BOUND), None, ALU.mult))
        chain(nc.vector.tensor_scalar(scal[:, 4:5], wc[:, 0, 4:5], 0.5 * H_BOUND, wc[:, 1, 4:5], ALU.mult, ALU.mult))
        chain(nc.vector.tensor_tensor(out=scal[:, 2:3], in0=scal[:, 4:5], in1=wc[:, 2, 4:5], op=ALU.mult))
        assert steps[0] == SCAL_READY, steps[0]

        def product(T, u, bufs):
            dve.wait_ge(up_full, T + 1)
            dve.wait_ge(silu_ready, T + 1)
            if not isinstance(T, int) or T >= 2:
                dve.wait_ge(hhi_ready, T - 1)
                dve.wait_ge(hlo_ready, T - 1)
            nc.vector.scalar_tensor_tensor(out=bufs["h"][u][:, :], in0=ps[:, UP, :], scalar=scal[:, 1:2],
                                           in1=bufs["silu"][u][:, :], op0=ALU.mult, op1=ALU.mult).then_inc(h_ready, 1)

        def h_lo(T, u, bufs):
            dve.wait_ge(hhi_ready, T + 1)
            dve.wait_ge(h_ready, T + 1)
            nc.vector.tensor_tensor(out=bufs["hs"][u][1][:, :], in0=bufs["h"][u][:, :], in1=bufs["hs"][u][0][:, :],
                                    op=ALU.subtract).then_inc(hlo_ready, 1)

        def residual(f, c):
            dve.wait_ge(down_full, f * CHUNKS * IT + (c + 1) * IT)
            if f == 1:
                dve.wait_ge(x2_ready, TPC * (c + 1))
            for j in range(TPC):
                xi = x[:, TPC * c + j, :]
                nc.vector.scalar_tensor_tensor(out=xi, in0=ps[:, DOWN + j, :], scalar=scal[:, 2:3], in1=xi,
                                               op0=ALU.mult, op1=ALU.add).then_inc(resid_ready, 1)

        def ffn(f, bufs):
            for c in range(CHUNKS):
                T0 = f * CHUNKS * IT + c * IT
                ln = (1, 2, 3, 4)[c] if f == 0 else (9, 10, 11, None)[c]
                for t in (0, 1):
                    product(T0 + t, t % 2, bufs)
                    if f == 0 and c == 0 and t == 0:
                        finish_weight(2, 7)
                    h_lo(T0 + t, t % 2, bufs)
                    if c and t == 0:
                        residual(f, c - 1)
                if ln is not None:
                    layer_norm(ln)
                if f == 0 and c == 1:
                    dve.wait_ge(wq_loaded, 16)
                    nc.vector.tensor_reduce(part[:, 3, 1:2], wq_raw[:, :], AX.X, ALU.max, apply_absolute_value=True)
                    nc.vector.memset(part[:, 3, 0:1], 0.0).then_inc(part_ready, 1)
                    dve.wait_ge(allr_ready, 8)
                    chain(nc.vector.tensor_copy(wc[:, 3, 1:2], allr[:, 3, 1:2]))
                    power_of_two(3)
                    chain(nc.vector.tensor_scalar(scal[:, 3:4], wc[:, 3, 4:5], 1.0 / XS, None, ALU.mult))
                    assert steps[0] == WQ_READY, steps[0]
                if f == 0 and c == 2:
                    dve.wait_ge(whi_ready, 16)
                    nc.vector.scalar_tensor_tensor(
                        out=wq[1][:, :, :].rearrange("p a b -> p (a b)"), in0=wq_raw[:, :], scalar=wc[:, 3, 3:4],
                        in1=wq[0][:, :, :].rearrange("p a b -> p (a b)"), op0=ALU.mult,
                        op1=ALU.subtract).then_inc(wlo_ready, 1)
                with dve.Fori(1, 6) as i:
                    for t in (0, 1):
                        T = i * 2 + (T0 + t)
                        product(T, t, bufs)
                        h_lo(T, t, bufs)
                for t in (IT - 2, IT - 1):
                    if t == IT - 2 and ln is not None:
                        for j in range(TPC):
                            ln_lo(ln, j)
                    product(T0 + t, t % 2, bufs)
                    h_lo(T0 + t, t % 2, bufs)
            residual(f, CHUNKS - 1)

        ffn(0, ffn1)

        dve.wait_ge(tables_loaded, 48)
        dve.wait_ge(spilled, 16)
        HALF = SEQ_PAIRS // 2

        def add_bias(i):
            b0 = 2 * (i % 2)
            dve.wait_ge(qkv_full, i + 1)
            if i >= 2:
                dve.wait_ge(v_ready, i - 1)
                dve.wait_ge(rot_ready, 3 * (i - 1))
            for s in range(2):
                nc.vector.scalar_tensor_tensor(
                    out=qkv_raw[i % 2][:, HALF * s:HALF * (s + 1), :].rearrange("p a b -> p (a b)"),
                    in0=ps[:, b0 + s, 0:QKV // 2], scalar=scal[:, 3:4], in1=bq[:, s * QKV // 2:(s + 1) * QKV // 2],
                    op0=ALU.mult, op1=ALU.add).then_inc(raw_ready, 1)

        st4 = store[:, :, :].rearrange("p (g t) c -> p g t c", t=SEQ_TILES)

        def rotate(i):
            b, tt = divmod(i, SEQ_TILES)
            dve.wait_ge(rot_ready, 3 * (i + 1))
            nc.vector.tensor_tensor(out=st4[:, SEQ_PAIRS * b:SEQ_PAIRS * (b + 1), tt, 0:QK], in0=rot_c[:, :, :],
                                    in1=rot_s[:, :, :], op=ALU.add).then_inc(qk_ready, 1)

        for i in range(TOKEN_TILES):
            m, j = divmod(i, TPC)
            if m < CHUNKS - 1 and j == 1:
                layer_norm(5 + m)
            if m < CHUNKS - 1 and j == 2:
                ln_lo(5 + m, 0)
                ln_lo(5 + m, 1)
            if m < CHUNKS - 1 and j == 3:
                ln_lo(5 + m, 2)
                ln_lo(5 + m, 3)
            add_bias(i)
            if i:
                rotate(i - 1)
        rotate(TOKEN_TILES - 1)

        dve.wait_ge(lnt_full, 32)
        for v in range(BUF):
            nc.vector.memset(ka[v][ROWS:MROWS, :], 1.0)
            chain(nc.vector.memset(vs[v][:, :, HEAD:32], 0.0))
            nc.vector.memset(vs[v][:, :, HEAD:HEAD + 1], 1.0).then_inc(ones_ready, 1)

        def reduce_piece(k, r):
            qt, k0, w, heads = PIECES[r]
            dve.wait_ge(p1_full, num(k) * NP_ + r + 1)
            dst = rowmax[:, qt, heads[0]:heads[-1] + 1] if k0 == 0 else rowmax2[:, qt - 4, heads[0]:heads[-1] + 1]
            nc.vector.tensor_reduce(dst, ps[:, PASS1 + r % 2, 0:w * len(heads)].rearrange("p (h w) -> p h w", w=w),
                                    AX.X, ALU.max).then_inc(p1_read, 1)

        def split_rowmax(k):
            dve.wait_ge(p1_read, num(k) * NP_ + NP_)
            hi = rowmax[:, SEQ_TILES // 2:, :]
            nc.vector.tensor_tensor(out=hi, in0=hi, in1=rowmax2[:, :, :], op=ALU.max).then_inc(max_step, 1)
            dve.wait_ge(max_step, num(k) * 4 + 1)
            if not never(k, 1):
                dve.wait_ge(mt_full, num(k))
            nc.vector.tensor_scalar(nm[:, :, 0, :], rowmax[:, :, :], -1.0, None, ALU.mult).then_inc(max_step, 1)
            dve.wait_ge(max_step, num(k) * 4 + 2)
            nc.vector.scalar_tensor_tensor(out=rest[:, :, :], in0=rowmax[:, :, :], scalar=-1.0, in1=nm[:, :, 0, :],
                                           op0=ALU.mult, op1=ALU.subtract).then_inc(max_step, 1)
            dve.wait_ge(max_step, num(k) * 4 + 3)
            nc.vector.tensor_copy(nm[:, :, 1, :], rest[:, :, :]).then_inc(max_step, 1)
            dve.wait_ge(max_step, num(k) * 4 + 4)
            nc.vector.tensor_tensor(out=nm[:, :, 2, :], in0=rest[:, :, :], in1=nm[:, :, 1, :],
                                    op=ALU.subtract).then_inc(nm_ready, 1)

        def take_rowmax(g):
            dve.wait_ge(mt_full, num(g) + 1)
            if not never(g, 1):
                dve.wait_ge(m_placed, num(g) * 48)
            nc.vector.tensor_copy(mrow[:, :], ps[0:3 * Q_PER_KV, SHARED_BANK, :].bitcast(BF16)).then_inc(mrow_ready, 1)

        def take_qk(g, h):
            dve.wait_ge(qkt_full, num(g) * 5 + h + 1)
            nc.vector.tensor_copy(qa[buf(g)][0:ROWS, h, :], ps[0:ROWS, SHARED_BANK, :].bitcast(BF16)).then_inc(qkt_dve, 1)

        def normalise(g, c):
            pair, odd = pair_of(g)
            dve.wait_ge(ctxt_full, num(g) * 2 + c + 1)
            if c or not never(g, 1):
                dve.wait_ge(norm_ready, num(g) * 2 + c)
            t = ps[:, SHARED_BANK, :].rearrange("p (t h d) -> p t h d", t=4, h=Q_PER_KV)
            nc.vector.reciprocal(rec[:, :, :], t[:, :, :, HEAD]).then_inc(rec_ready, 1)
            dve.wait_ge(rec_ready, num(g) * 2 + c + 1)
            dst = store[:, bass.ds(pair * SEQ_TILES + 4 * c, 4), QW * odd:QW * (odd + 1)].rearrange("p t (h d) -> p t h d", d=HEAD)
            nc.vector.tensor_tensor(out=dst, in0=t[:, :, :, 0:HEAD],
                                    in1=rec[:, :, :].unsqueeze(3).to_broadcast([P, 4, Q_PER_KV, HEAD]),
                                    op=ALU.mult).then_inc(norm_ready, 1)

        def body(k, first, second, ahead, tail):
            for s in range(NU):
                if s == 0:
                    for r in range(LEAD):
                        if r == ROWMAX_AT and second:
                            take_rowmax(shift(k, -1))
                        if first:
                            reduce_piece(k, r)
                if first:
                    for r in SLOTS[s]:
                        reduce_piece(k, r)
                use = SHARED.get(s)
                if use == ("ctx", 1) and tail:
                    normalise(shift(k, -2), 1)
                elif use == ("ctx", 0) and second:
                    normalise(shift(k, -1), 0)
                elif use and use[0] == "qk" and use[1] in QK_ON_DVE and ahead:
                    take_qk(shift(k, 1), use[1])
            if first:
                split_rowmax(k)

        for h in QK_ON_DVE:
            take_qk((None, 0), h)
        for k in (0, 1):
            body((None, k), True, k >= 1, True, False)
        with dve.Fori(0, 3) as i:
            for u in range(BUF):
                body((i, u + 2), True, True, True, True)
        for k in (14, 15, 16):
            body((None, k), k < GROUPS, True, k + 1 < GROUPS, True)
        normalise((None, GROUPS - 1), 1)

        dve.wait_ge(wd_loaded, 32)

        def bias_x(i):
            nc.vector.tensor_tensor(out=x[:, i, :], in0=x[:, i, :], in1=bd[:, :], op=ALU.add).then_inc(bias_ready, 1)

        bias_x(0)
        for i in range(TOKEN_TILES):
            if i + 1 < TOKEN_TILES:
                bias_x(i + 1)
            dve.wait_ge(dense_full, i + 1)
            dve.wait_ge(bias_ready, i + 1)
            nc.vector.tensor_tensor(out=x[:, i, :], in0=ps[:, i % 2, :], in1=x[:, i, :], op=ALU.add).then_inc(x2_ready, 1)
            if i == 8:
                layer_norm(8)
            if i in (12, 13):
                ln_lo(8, 2 * (i - 12))
                ln_lo(8, 2 * (i - 12) + 1)
        ffn(1, ffn2)

    @block.tensor
    def _(pe):
        mm, tr = nc.tensor.matmul, nc.tensor.transpose
        PASSES = ((0, 0), (0, 1), (1, 0))

        def ln_transpose(n, j):
            q = TPC * n + j
            pe.wait_ge(xnorm_ready, q + 1)
            if q >= 2:
                pe.wait_ge(xlo_ready, q - 1)
            for h in range(HB):
                last = tr(ps[:, LNT + j % 2, h * P:(h + 1) * P], xnorm[j][:, h * P:(h + 1) * P], ident[:, :])
            last.then_inc(lnt_full, 1)

        def up_product(bank, w, xt, t, full):
            for k in range(HB):
                for n, (a, b) in enumerate(PASSES):
                    last = mm(ps[:, bank, :], w[a][:, k, bass.ts(t, P)], xt[b][:, k, :],
                              start=(k == 0 and n == 0), stop=(k == HB - 1 and n == 2))
            last.then_inc(full, 1)

        def gate(T, t, w, xt):
            if not isinstance(T, int) or T:
                pe.wait_ge(silu_ready, T)
            up_product(GATE, w, xt, t, gate_full)

        def up(T, t, w, xt):
            if not isinstance(T, int) or T:
                pe.wait_ge(h_ready, T)
            up_product(UP, w, xt, t, up_full)

        def down(T, t, u, w, bufs, first, last_tile):
            pe.wait_ge(hhi_ready, T + 1)
            pe.wait_ge(hlo_ready, T + 1)
            hs = bufs["hs"][u]
            for j in range(TPC):
                for n, (a, b) in enumerate(PASSES):
                    last = mm(ps[:, DOWN + j, :], hs[a][:, j * P:(j + 1) * P], w[b][:, t, :],
                              start=(first and n == 0), stop=(last_tile and n == 2))
            last.then_inc(down_full, 1)

        def ffn(f, bufs, wa, wb, wc_):
            T_last = None
            for c in range(CHUNKS):
                T0 = f * CHUNKS * IT + c * IT
                n = c + 8 * f
                xt = xt_of(n)
                ln = (1, 2, 3, 4)[c] if f == 0 else (9, 10, 11, None)[c]
                pe.wait_ge(xhi_ready, TPC * (n + 1))
                pe.wait_ge(xlo_ready, TPC * (n + 1))
                for t in (0, 1):
                    if f == 0 and c == 0 and t == 0:
                        pe.wait_ge(whi_ready, 4)
                        pe.wait_ge(wlo_ready, 4)
                    gate(T0 + t, t, wa, xt)
                    if f == 0 and c == 0 and t == 0:
                        pe.wait_ge(whi_ready, 8)
                        pe.wait_ge(wlo_ready, 8)
                    up(T0 + t, t, wb, xt)
                    if t == 1:
                        if f == 0 and c == 0:
                            pe.wait_ge(whi_ready, 15)
                            pe.wait_ge(wlo_ready, 15)
                        if c:
                            pe.wait_ge(resid_ready, TPC * (CHUNKS * f + c))
                        down(T0, 0, 0, wc_, bufs, True, False)
                    elif c:
                        down(T0 - 1, IT - 1, 1, wc_, bufs, False, True)
                with pe.Fori(1, 6) as i:
                    for t in (0, 1):
                        T = i * 2 + (T0 + t)
                        gate(T, i * 2 + t, wa, xt)
                        up(T, i * 2 + t, wb, xt)
                        down(T - 1, i * 2 + (t - 1), 1 - t, wc_, bufs, False, False)
                for t in (IT - 2, IT - 1):
                    if t == IT - 2 and ln is not None:
                        ln_transpose(ln, 0)
                        ln_transpose(ln, 1)
                    gate(T0 + t, t, wa, xt)
                    if t == IT - 2 and ln is not None:
                        ln_transpose(ln, 2)
                        ln_transpose(ln, 3)
                    up(T0 + t, t, wb, xt)
                    down(T0 + t - 1, t - 1, (t - 1) % 2, wc_, bufs, False, False)
            down((f + 1) * CHUNKS * IT - 1, IT - 1, 1, wc_, bufs, False, True)

        pe.wait_ge(consts_ready, 3)
        for j in range(TPC):
            ln_transpose(0, j)
        ffn(0, ffn1, w1s, w3s, w2s)

        def qkv(i):
            m, j = divmod(i, TPC)
            xt = xt_of(4 + m)
            if i == 0:
                pe.wait_ge(silu_ready, CHUNKS * IT)
                pe.wait_ge(h_ready, CHUNKS * IT)
                pe.wait_ge(whi_ready, 16)
                pe.wait_ge(wlo_ready, 16)
            if i == 1:
                pe.wait_ge(resid_ready, TOKEN_TILES)
            if i >= 2:
                pe.wait_ge(raw_ready, 2 * (i - 1))
            if j == 0:
                pe.wait_ge(xhi_ready, TPC * (5 + m))
                pe.wait_ge(xlo_ready, TPC * (5 + m))
            for s in range(2):
                for k in range(HB):
                    for n, (a, b) in enumerate(PASSES):
                        last = mm(ps[:, 2 * (i % 2) + s, 0:QKV // 2], xt[a][:, k, j * P:(j + 1) * P],
                                  wq[b][:, k, s * QKV // 2:(s + 1) * QKV // 2],
                                  start=(k == 0 and n == 0), stop=(k == HB - 1 and n == 2))
            last.then_inc(qkv_full, 1)

        for i in range(TOKEN_TILES):
            m, j = divmod(i, TPC)
            if m < CHUNKS - 1 and j == 2:
                ln_transpose(5 + m, 0)
                ln_transpose(5 + m, 1)
            if m < CHUNKS - 1 and j == 3:
                ln_transpose(5 + m, 2)
                ln_transpose(5 + m, 3)
            qkv(i)

        def shared_free(k, use, second, ahead, tail):
            happens = {"rowmax": second, ("ctx", 1): tail, ("ctx", 0): second}
            before = [o for o in ORDER[:ORDER.index(use)] if happens.get(o, ahead)]
            n = num(k)
            if before:
                o = before[-1]
            elif never(k, GROUPS):
                o, n = ("qk", 4), num(k) - 1
            elif k[0] is None and k[1] >= GROUPS:
                o, n = ("ctx", 0), num(k) - 1
            else:
                o, n = ("qk", 4), n - 1
            if o == "rowmax":
                pe.wait_ge(mrow_ready, n)
            elif o == ("ctx", 1):
                pe.wait_ge(norm_ready, n * 2 - 2)
            elif o == ("ctx", 0):
                pe.wait_ge(norm_ready, n * 2 - 1)
            elif o[1] in QK_ON_DVE:
                pe.wait_ge(qkt_dve, n + 2)
            else:
                pe.wait_ge(qkt_act, n * 4 + 4 + o[1])

        def transpose_qk(g, h):
            if h == 0:
                pe.wait_ge(split_step, num(g) * NSPLIT + NSPLIT)
            bank = ps[0:ROWS, SHARED_BANK, :].bitcast(BF16)
            for tt in range(SEQ_TILES):
                src = parts_k[g[1] % 2][:, tt, :] if h == 4 else parts_q[g[1] % 2][:, Q_PER_KV * tt + h, :]
                last = tr(bank[:, tt * P:(tt + 1) * P], src, ident16[:, :])
            last.then_inc(qkt_full, 1)

        def score_piece(k, r):
            qt, k0, w, heads = PIECES[r]
            v = buf(k)
            if r >= 2 or not never(k, 1):
                pe.wait_ge(p1_read, num(k) * NP_ + (r - 1))
            if r == 0:
                pe.wait_ge(qkt_act, num(k) * 4 + 4)
                pe.wait_ge(qkt_dve, num(k) + 1)
            diagonal = k0 + w == P * (qt + 1)
            for n, h in enumerate(heads):
                last = mm(ps[:, PASS1 + r % 2, n * w:(n + 1) * w], qa[v][0:ROWS, h, qt * P:(qt + 1) * P],
                          ka[v][0:ROWS, k0:k0 + w], start=True, stop=not diagonal)
                if diagonal:
                    last = mm(ps[:, PASS1 + r % 2, (n + 1) * w - P:(n + 1) * w], ident16[:, :], negmask[:, :],
                              start=False, stop=True)
            last.then_inc(p1_full, 1)

        def transpose_rowmax(g):
            pe.wait_ge(nm_ready, num(g) + 1)
            bank = ps[0:3 * Q_PER_KV, SHARED_BANK, :].bitcast(BF16)
            for qt in range(SEQ_TILES):
                last = tr(bank[:, qt * P:(qt + 1) * P], nm[:, qt, :, :].rearrange("p a b -> p (a b)"), ident16[:, :])
            last.then_inc(mt_full, 1)

        def scores_t(g, u, pair):
            q0, q1, _ = unit_cols(u)
            kt = UNITS[u][1]
            U, v = num(g) * NU + u, buf(g)
            if u == 0 and pair == 0:
                pe.wait_ge(m_placed, num(g) * 48 + 48)
            if u or not never(g, 1):
                pe.wait_ge(exp_ready, U * 2 + (pair - 1))
            for h in (2 * pair, 2 * pair + 1):
                last = mm(ps[:, h, 0:q1 - q0], ka[v][0:MROWS, kt * P:(kt + 1) * P], qa[v][0:MROWS, h, q0:q1],
                          start=True, stop=True)
            last.then_inc(st_full, 1)

        def values(g, u):
            c, kt = UNITS[u]
            q0, q1, at = unit_cols(u)
            v = buf(g)
            pe.wait_ge(exp_ready, (num(g) * NU + u) * 2 + 2)
            if u in DIAGONAL:
                pe.wait_ge(diag_ready, num(g) * ND + DIAGONAL.index(u) + 1)
            if u == 0:
                pe.wait_ge(vs_ready, num(g) + 1)
            first = u in (0, 4)
            if first and (c or not never(g, 1)):
                pe.wait_ge(ctx_ready, num(g) * 2 + c)
            for h in range(Q_PER_KV):
                last = mm(ps[32 * h:32 * h + 32, CTX_BANK, at:512], vs[v][:, kt, :], probs[u % PBUF][:, h, 0:q1 - q0],
                          start=first, stop=u in (3, NU - 1))
            last.then_inc(pv_full, 1)

        def transpose_context(g, c):
            pe.wait_ge(ctx_ready, num(g) * 2 + c + 1)
            for j in range(4):
                last = tr(ps[:, SHARED_BANK, j * P:(j + 1) * P], ctx_sb[:, j * P:(j + 1) * P], ident[:, :])
            last.then_inc(ctxt_full, 1)

        def body(k, first, second, ahead, tail):
            flags = second, ahead, tail
            for s in range(NU):
                if s == 0:
                    for r in range(LEAD):
                        if r == TAIL_AT and tail:
                            values(shift(k, -2), NU - 1)
                        if r == ROWMAX_AT and second:
                            shared_free(k, "rowmax", *flags)
                            transpose_rowmax(shift(k, -1))
                        if first:
                            score_piece(k, r)
                todo = list(SLOTS[s]) if first else []
                if second:
                    scores_t(shift(k, -1), s, 0)
                for r in todo[:1]:
                    score_piece(k, r)
                if second:
                    scores_t(shift(k, -1), s, 1)
                for r in todo[1:2]:
                    score_piece(k, r)
                if second and s:
                    values(shift(k, -1), s - 1)
                for r in todo[2:]:
                    score_piece(k, r)
                use = SHARED.get(s)
                if use and use[0] == "qk" and ahead:
                    shared_free(k, use, *flags)
                    transpose_qk(shift(k, 1), use[1])
                elif use == ("ctx", 1) and tail:
                    shared_free(k, use, *flags)
                    transpose_context(shift(k, -2), 1)
                elif use == ("ctx", 0) and second:
                    shared_free(k, use, *flags)
                    transpose_context(shift(k, -1), 0)

        pe.wait_ge(ones_ready, BUF)
        pe.wait_ge(raw_ready, 2 * TOKEN_TILES)
        pe.wait_ge(xlo_ready, TPC * 8)
        for h in range(5):
            if h == 1:
                pe.wait_ge(qkt_dve, 1)
            elif h:
                pe.wait_ge(qkt_act, h - 1)
            transpose_qk((None, 0), h)
        for k in (0, 1):
            body((None, k), True, k >= 1, True, False)
        with pe.Fori(0, 3) as i:
            for u in range(BUF):
                body((i, u + 2), True, True, True, True)
        for k in (14, 15, 16):
            body((None, k), k < GROUPS, True, k + 1 < GROUPS, True)
        values((None, GROUPS - 1), NU - 1)
        pe.wait_ge(norm_ready, 2 * GROUPS - 1)
        transpose_context((None, GROUPS - 1), 1)

        st4 = store[:, :, :].rearrange("p (g t) c -> p g t c", t=SEQ_TILES)

        def transpose_rows(i):
            b, tt = divmod(i, SEQ_TILES)
            if i >= 2:
                pe.wait_ge(ctx_t_ready, i - 1)
            for q in range(HB):
                last = tr(ps[:, 4 + i % 2, q * P:(q + 1) * P], st4[:, SEQ_PAIRS * b + q, tt, 0:2 * QW], ident[:, :])
            last.then_inc(dt_full, 1)

        def project(i):
            pe.wait_ge(ctx_t_ready, i + 1)
            if i >= 2:
                pe.wait_ge(x2_ready, i - 1)
            for q in range(HB):
                last = mm(ps[:, i % 2, :], ctx_t[i % 2][:, q, :], wd[:, q, :], start=(q == 0), stop=(q == HB - 1))
            last.then_inc(dense_full, 1)

        pe.wait_ge(norm_ready, 2 * GROUPS)
        pe.wait_ge(wd_loaded, 32)
        pe.wait_ge(exp_ready, 2 * NU * GROUPS)
        pe.wait_ge(ctx_ready, 2 * GROUPS)
        transpose_rows(0)
        for i in range(TOKEN_TILES):
            if i + 1 < TOKEN_TILES:
                transpose_rows(i + 1)
            if i in (12, 13):
                ln_transpose(8, 2 * (i - 12))
                ln_transpose(8, 2 * (i - 12) + 1)
            project(i)
        pe.wait_ge(x2_ready, TOKEN_TILES)
        pe.wait_ge(w13_back, 16)
        pe.wait_ge(w2_back, 16)
        ffn(1, ffn2, w1b, w3b, w2b)

    ctx.close()


LN_STEPS = 4 + 4 + 3 + 12 + 1
WEIGHT_STEPS = 2 + 6
SCAL_READY = LN_STEPS + 3 * WEIGHT_STEPS + 4
WQ_READY = SCAL_READY + 2 * LN_STEPS + 1 + 6 + 1


def rotation_tables():
    inv = (1.0 / np.float32(1000000.0) ** (np.arange(0, HEAD, 2, dtype=np.float32) / np.float32(HEAD))).astype(np.float32)
    f = np.outer(np.arange(SEQ, dtype=np.float32), inv).astype(np.float32)
    c, s = np.cos(f).astype(np.float32), np.sin(f).astype(np.float32)
    return np.concatenate([c, c], 1), np.concatenate([-s, s], 1)


def kernel(**inputs):
    import concourse.bacc as bacc
    from concourse.bass_utils import run_bass_kernel_spmd

    def t(name):
        return np.ascontiguousarray(np.asarray(inputs[name]).T)

    def by_pair(a):
        a = a.reshape(a.shape[:-1] + (SEQ_PAIRS, 2, QKV // KV_HEADS))
        cut = [a[..., lo:hi].reshape(a.shape[:-2] + (-1,)) for lo, hi in ((0, QW), (QW, QW + HEAD), (QW + HEAD, QW + 2 * HEAD))]
        return np.ascontiguousarray(np.concatenate(cut, -1).reshape(a.shape[:-3] + (QKV,)))

    cos, sin = rotation_tables()
    arrays = {
        "x_in": np.ascontiguousarray(inputs["L0_attn_hidden_states"]).reshape(BATCH * SEQ, HID),
        "w1t": t("L0_ffn_w1"), "m1t": t("L0_ffn_mean_w1"), "w3t": t("L0_ffn_w3"), "m3t": t("L0_ffn_mean_w3"),
        "w2t": t("L0_ffn_w2"), "m2t": t("L0_ffn_mean_w2"), "wqkvt": by_pair(t("L0_attn_w_qkv")),
        "b_qkv": by_pair(np.asarray(inputs["L0_attn_b_qkv"])), "wdt": t("L0_attn_w_dense"),
        "b_d": np.ascontiguousarray(inputs["L0_attn_b_dense"]), "cos_in": cos, "sin_in": sin,
    }
    nc = bacc.Bacc("TRN2", target_bir_lowering=False, num_devices=1)
    args = [nc.dram_tensor(n, a.shape, mybir.dt.from_np(a.dtype), kind="ExternalInput").ap() for n, a in arrays.items()]
    args.append(nc.dram_tensor("y_out", (BATCH * SEQ, HID), F32, kind="ExternalOutput").ap())
    build(nc, *args)
    r = run_bass_kernel_spmd(nc, [arrays], core_ids=[0])
    return r.results[0]["y_out"].reshape(BATCH, SEQ, HID)
```

```python
import numpy as np

import concourse.bass as bass
from concourse import mybir

F32 = mybir.dt.float32
F16 = mybir.dt.float16
BF16 = mybir.dt.bfloat16
I32 = mybir.dt.int32
I8 = mybir.dt.int8
ALU = mybir.AluOpType
ACT = mybir.ActivationFunctionType
AX = mybir.AxisListType

P = 128
BATCH, SEQ, HID, INTER = 2, 1024, 512, 1792
HEAD, KV_HEADS, Q_PER_KV = 16, 8, 4
TOKEN_TILES = BATCH * SEQ // P
SEQ_TILES = SEQ // P
HB = HID // P
IT = INTER // P
CHUNK = 512
TPC = CHUNK // P
CHUNKS = TOKEN_TILES // TPC
GROUPS = BATCH * KV_HEADS
PAIRS = GROUPS // 2
SEQ_PAIRS = KV_HEADS // 2
QW = Q_PER_KV * HEAD
QK = 2 * (QW + HEAD)
GW = QK + 2 * HEAD
QKV = SEQ_PAIRS * GW
ROWS = 6 * HEAD
MROWS = ROWS + 3
SM_SCALE = 1.0 / HEAD
EPS = 1e-5
XS = 1024.0
H_BOUND = 2.0 ** 33
NEG = -3.0e38
RSQRT_SEED = 0x5F3759DF
BUF = 4
PBUF = 3

def rotated(i):
    return 3 * (i + 1) - max(0, i + 1 - SEQ_TILES)


UNITS = [(0, kt) for kt in (0, 1, 2, 3)] + [(1, kt) for kt in (0, 4, 5, 6, 7, 1, 2, 3)]
NU = len(UNITS)
DIAGONAL = [u for u, (c, kt) in enumerate(UNITS) if kt >= 4 * c]
ND = len(DIAGONAL)


NSPLIT = 8


def score_pieces():
    out = []
    for qt in reversed(range(SEQ_TILES)):
        width = P * (qt + 1)
        for k0 in range(0, width, 512):
            w = min(512, width - k0)
            nh = max(1, min(Q_PER_KV, 512 // w))
            out += [(qt, k0, w, list(range(h, h + nh))) for h in range(0, Q_PER_KV, nh)]
    return out


PIECES = score_pieces()
NP_ = len(PIECES)
TAILS = 3


def piece_slots():
    cols = [512 * (c + 1) - max(512 * c, P * kt) for c, kt in UNITS[NU - TAILS:] + UNITS[:NU - TAILS]]
    total, at, out = float(sum(cols)), 0.0, []
    done = 0
    for n in cols:
        at += n
        upto = int(round(NP_ * at / total))
        out.append(list(range(done, upto)))
        done = upto
    return out


SLOTS = piece_slots()
SHARED = {0: ("rowmax", 0), 1: ("qk", 0), 3: ("qk", 1), 4: ("ctx", 1), 5: ("qk", 2), 6: ("qk", 3), 8: ("ctx", 0),
          10: ("qk", 4)}
ORDER = [SHARED[s] for s in sorted(SHARED)]
REPEAT_AT = 9
EARLY = SEQ_TILES + 4
QK_ON_DVE = (0,)
QK_ON_ACT = (1, 2, 3, 4)


def num(k):
    i, c = k
    return c if i is None else i * BUF + c


def shift(k, by):
    return k[0], k[1] + by


def buf(k):
    return k[1] % BUF


def unit_at(k, s, second, tail):
    if s < TAILS:
        return (shift(k, -2), NU - TAILS + s) if tail else None
    return (shift(k, -1), s - TAILS) if second else None


def unit_before(k, s, second, tail):
    if s == 0:
        return (shift(k, -2), NU - TAILS - 1) if tail else None
    if s == TAILS and not tail:
        return None
    return unit_at(k, s - 1, second, tail)


def pair_of(k):
    i, c = k
    return (c // 2 if i is None else i * (BUF // 2) + c // 2), c % 2


def never(k, least=0):
    return k[0] is None and k[1] < least


def unit_cols(u):
    c, kt = UNITS[u]
    q0 = max(512 * c, P * kt)
    return q0, 512 * (c + 1), q0 - 512 * c


def build(nc, x_in, w1t, m1t, w3t, m3t, w2t, m2t, wqkvt, b_qkv, wdt, b_d, cos_in, sin_in, out):
    from contextlib import ExitStack
    RADD, RMAX = bass.bass_isa.ReduceOp.add, bass.bass_isa.ReduceOp.max

    ctx = ExitStack()
    base = 16512

    def at(name, shape, dt, offset):
        return nc.alloc_sbuf_tensor_at(name, shape, dt, offset=base + offset)

    W_T = HB * INTER * 2
    A0 = 0
    w_all = at("w_all", [P, 3 * W_T], F16, A0)

    def halves(t, at_, a):
        return [t[:, at_ // 2 + i * W_T // 2:at_ // 2 + (i + 1) * W_T // 2].rearrange("p (a b) -> p a b", a=a)
                for i in range(2)]

    w1s, w3s, w2s = halves(w_all, 0, HB), halves(w_all, 2 * W_T, HB), halves(w_all, 4 * W_T, IT)
    X0 = 6 * W_T
    x = at("x", [P, TOKEN_TILES, HID], F32, X0)
    B0 = X0 + TOKEN_TILES * HID * 4
    SLOT = HB * INTER * 5
    wbase = [at(f"wbase{i}", [P, HB * INTER], F32, B0 + i * SLOT) for i in range(2)]
    wsign = [at(f"wsign{i}", [P, HB * INTER], I8, B0 + i * SLOT + HB * INTER * 4) for i in range(2)]
    C0 = B0 + SLOT
    D0 = C0 + SLOT
    w_raw = at("w_raw", [P, 3, HB * INTER], F32, A0)

    def working(tag, offset):
        return {
            "silu": [at(f"silu{tag}{i}", [P, CHUNK], F32, offset + i * 2048) for i in range(2)],
            "h": [at(f"h{tag}{i}", [P, CHUNK], F32, offset + 4096 + i * 2048) for i in range(2)],
            "hs": [[at(f"h{n}{tag}{i}", [P, CHUNK], F16, offset + 8192 + (2 * i + j) * 1024)
                    for j, n in enumerate(("hi", "lo"))] for i in range(2)],
        }

    ffn1 = working("a", C0 + 8192)
    xt0 = [at("xt0_hi", [P, HB, CHUNK], F16, D0), at("xt0_lo", [P, HB, CHUNK], F16, D0 + 4096)]
    xt1 = [at("xt1_hi", [P, HB, CHUNK], F16, C0), at("xt1_lo", [P, HB, CHUNK], F16, C0 + 4096)]
    xnorm = [at(f"xnorm{i}", [P, HID], F32, D0 + 8192 + i * 2048) for i in range(TPC)]
    K0 = D0 + 16384
    ident = at("ident", [P, P], F32, K0)
    ident16 = at("ident16", [P, P], BF16, K0 + 512)
    negmask = at("negmask", [P, P], BF16, K0 + 768)
    cos = at("cos", [P, SEQ_TILES, HEAD], F32, K0 + 1024)
    sin = at("sin", [P, SEQ_TILES, HEAD], F32, K0 + 1536)
    stats = at("stats", [P, TPC, 6], F32, K0 + 2048)
    mean_var = at("mean_var", [P, 4, TPC, 2], F32, K0 + 3136)
    rstd = at("rstd", [P, 4, TPC], F32, K0 + 3264)
    nw = at("nw", [P, 4, TPC], F32, K0 + 2176)
    dabs = at("dabs", [P, 16], F32, K0 + 2240)
    bmax = at("bmax", [P, 16], F32, K0 + 2304)
    part = at("part", [P, 4, 2], F32, K0 + 2368)
    allr = at("allr", [P, 4, 2], F32, K0 + 2400)
    wc = at("wc", [P, 4, 6], F32, K0 + 2432)
    scal = at("scal", [P, 8], F32, K0 + 2528)
    rec = at("rec", [P, 4, Q_PER_KV], F32, K0 + 2560)
    rowmax = at("rowmax", [P, SEQ_TILES, Q_PER_KV], F32, K0 + 2624)
    rowmax2 = at("rowmax2", [P, SEQ_TILES // 2, Q_PER_KV], F32, K0 + 2752)
    rest = at("rest", [P, SEQ_TILES, Q_PER_KV], F32, K0 + 2816)
    nm = at("nm", [P, SEQ_TILES, 3, Q_PER_KV], BF16, K0 + 2944)
    assert base + K0 + 3328 <= 229368

    wq = [at("wq_hi", [P, HB, QKV], F16, B0), at("wq_lo", [P, HB, QKV], F16, B0 + 6144)]
    wq_raw = at("wq_raw", [P, HB * QKV], F32, B0 + 12288)
    R0 = C0 + 20480
    qkv_raw = [at(f"qkv_raw{i}", [P, SEQ_PAIRS, GW], F32, R0 + i * 3072) for i in range(2)]
    rot_c = at("rot_c", [P, SEQ_PAIRS, QK], F32, R0 + 6144)
    rot_s = at("rot_s", [P, SEQ_PAIRS, QK], F32, R0 + 8704)
    bq = at("bq", [P, QKV], F32, R0 + 11264)
    store = at("store", [P, PAIRS * SEQ_TILES, GW], F32, 0)
    S1 = PAIRS * SEQ_TILES * GW * 4
    qa = [at(f"qa{i}", [P, Q_PER_KV, SEQ], BF16, S1 + i * 8192) for i in range(BUF)]
    ctx_sb = at("ctx_sb", [P, 512], F32, S1 + BUF * 8192)
    assert S1 + BUF * 8192 + 2048 <= X0
    probs = [at(f"probs{i}", [P, Q_PER_KV, 512], F32, B0 + i * 8192) for i in range(PBUF)]
    E0 = B0 + PBUF * 8192
    W0, V0 = C0 + 8192, C0
    parts_at = (E0, W0)
    parts_q = [at(f"parts_q{i}", [P, SEQ_TILES * Q_PER_KV, ROWS], BF16, a) for i, a in enumerate(parts_at)]
    parts_k = [at(f"parts_k{i}", [P, SEQ_TILES, ROWS], BF16, a + 6144) for i, a in enumerate(parts_at)]
    left = at("left", [P, SEQ_TILES, QW + HEAD], F32, E0 + 7680)
    ka = [at(f"ka{i}", [P, SEQ], BF16, a) for i, a in enumerate((W0 + 7680, W0 + 9728, V0, V0 + 2048))]
    vs = [at(f"vs{i}", [P, SEQ_TILES, 32], F32, V0 + 4096 + i * 1024) for i in range(BUF)]
    mrow = at("mrow", [3 * Q_PER_KV, SEQ], BF16, D0)
    assert E0 + 10240 <= C0 and BUF * 1024 + 4096 <= 8192 and W0 + 11776 <= C0 + 20480
    wd = at("wd", [P, HB, HID], F32, B0 + 57344)
    bd = at("bd", [P, HID], F32, B0 + 57344 + 8192)
    ctx_t = [at(f"ctx_t{i}", [P, HB, P], F32, B0 + 57344 + 10240 + i * 2048) for i in range(2)]
    assert B0 + 57344 + 14336 == D0
    w2b_all = at("w2b_all", [P, W_T], F16, S1)
    w13b_all = at("w13b_all", [P, 2 * W_T], F16, B0)
    w1b, w3b, w2b = halves(w13b_all, 0, HB), halves(w13b_all, 2 * W_T, HB), halves(w2b_all, 0, IT)
    ffn2 = working("b", 8192)
    xt1b = [at("xt1b_hi", [P, HB, CHUNK], F16, 0), at("xt1b_lo", [P, HB, CHUNK], F16, 4096)]

    ps = ctx.enter_context(nc.psum_tensor("ps", [P, 8, 512], F32))
    GATE, UP, DOWN, LNT = 0, 1, 2, 6
    CTX_BANK, PASS1, SHARED_BANK = 4, 5, 7

    spill = nc.dram_tensor("spill", [P, 6 * W_T // 2], F16)

    def sem(name):
        return ctx.enter_context(nc.semaphore(name))

    x_loaded = [sem(f"x_loaded{i}") for i in range(CHUNKS)]
    w_loaded = [sem(f"w_loaded{i}") for i in range(15)]
    tables_loaded, wq_loaded, wd_loaded = sem("tables_loaded"), sem("wq_loaded"), sem("wd_loaded")
    spilled, w2_back, w13_back = sem("spilled"), sem("w2_back"), sem("w13_back")
    consts_ready = sem("consts_ready")
    ones_ready = sem("ones_ready")
    diff_ready = sem("diff_ready")
    sign_ready = sem("sign_ready")
    bmax_ready = sem("bmax_ready")
    part_ready = sem("part_ready")
    allr_ready = sem("allr_ready")
    weff_ready = sem("weff_ready")
    whi_ready, wlo_ready = sem("whi_ready"), sem("wlo_ready")
    dve_chain = sem("dve_chain")
    pool_chain = sem("pool_chain")
    xnorm_ready = sem("xnorm_ready")
    lnt_full = sem("lnt_full")
    xhi_ready, xlo_ready = sem("xhi_ready"), sem("xlo_ready")
    gate_full, up_full, down_full = sem("gate_full"), sem("up_full"), sem("down_full")
    silu_ready, h_ready = sem("silu_ready"), sem("h_ready")
    hhi_ready, hlo_ready = sem("hhi_ready"), sem("hlo_ready")
    resid_ready = sem("resid_ready")
    out_stored = sem("out_stored")
    qkv_full, raw_ready = sem("qkv_full"), sem("raw_ready")
    rot_ready, qk_ready, v_ready = sem("rot_ready"), sem("qk_ready"), sem("v_ready")
    split_step = sem("split_step")
    dup_ready = sem("dup_ready")
    pool_waited, vs_ready = sem("pool_waited"), sem("vs_ready")
    qkt_full = sem("qkt_full")
    qkt_dve, qkt_act = sem("qkt_dve"), sem("qkt_act")
    p1_full, p1_read = sem("p1_full"), sem("p1_read")
    max_step = sem("max_step")
    nm_ready, mt_full, mrow_ready, m_placed = sem("nm_ready"), sem("mt_full"), sem("mrow_ready"), sem("m_placed")
    st_full, exp_ready, diag_ready, pv_full = sem("st_full"), sem("exp_ready"), sem("diag_ready"), sem("pv_full")
    ctx_ready, ctxt_full, rec_ready, norm_ready = sem("ctx_ready"), sem("ctxt_full"), sem("rec_ready"), sem("norm_ready")
    dt_full, ctx_t_ready, dense_full, bias_ready, x2_ready = (
        sem("dt_full"), sem("ctx_t_ready"), sem("dense_full"), sem("bias_ready"), sem("x2_ready"))

    block = ctx.enter_context(nc.Block())

    WEIGHTS = [(w1s, 0, 0, 4, INTER), (w3s, 1, 4, 4, INTER), (w2s, 0, 8, 7, 2 * HID)]

    def slice_of(w, t, p):
        if w < 2:
            return t.rearrange("p (a b) -> p a b", a=HB)[:, :, 2 * P * p:2 * P * (p + 1)]
        return t.rearrange("p (a b) -> p a b", a=IT)[:, 2 * p:2 * p + 2, :]

    def half(w, j, p):
        return slice_of(w, WEIGHTS[w][0][j].rearrange("p a b -> p (a b)"), p)

    def x_tiles_ready(eng, n):
        if n < 4:
            eng.wait_ge(x_loaded[n], 16)
        elif n < 8:
            eng.wait_ge(resid_ready, TPC * (n - 4) + TPC)
        else:
            eng.wait_ge(x2_ready, TPC * (n - 8) + TPC)

    def xt_of(n):
        return xt0 if n % 2 == 0 else (xt1b if n >= 8 else xt1)

    @block.sync
    def _(sp):
        x_rows = x_in.rearrange("(n p) h -> p n h", p=P)
        out_rows = out.rearrange("(n p) h -> p n h", p=P)

        def load_x(c):
            sp.dma_start(x[:, TPC * c:TPC * (c + 1), :], x_rows[:, TPC * c:TPC * (c + 1), :]).then_inc(x_loaded[c], 16)

        load_x(0)
        sources = [(w1t, m1t), (w3t, m3t), (w2t, m2t)]

        def load_piece(w, p, which):
            _, slot, first, n, cols = WEIGHTS[w]
            src = sources[w][which].rearrange("(t p) n -> p t n", p=P)
            per = cols // src.shape[2]
            to = w_raw[:, w, p * cols:(p + 1) * cols] if which == 0 else wbase[slot][:, p * cols:(p + 1) * cols]
            sp.dma_start(to.rearrange("p (t n) -> p t n", t=per), src[:, per * p:per * (p + 1), :])\
                .then_inc(w_loaded[first + p], 16)

        for w in (0, 1):
            for p in range(4):
                load_piece(w, p, 1)
                load_piece(w, p, 0)
        for p in range(7):
            load_piece(2, p, 0)
        sp.wait_ge(wlo_ready, SLICES)
        for p in range(7):
            load_piece(2, p, 1)
        for c in range(1, CHUNKS):
            load_x(c)
        cs = [t.rearrange("(n p) d -> p n d", p=P) for t in (cos_in, sin_in)]
        sp.dma_start(cos[:, :, :], cs[0]).then_inc(tables_loaded, 16)
        sp.dma_start(sin[:, :, :], cs[1]).then_inc(tables_loaded, 16)
        sp.wait_ge(whi_ready, 3 * SLICES)
        sp.wait_ge(wlo_ready, 3 * SLICES)
        sp.dma_start(spill.ap(), w_all[:, :]).then_inc(spilled, 16)
        sp.dma_start(wq_raw[:, :].rearrange("p (t n) -> p t n", t=HB), wqkvt.rearrange("(t p) n -> p t n", p=P))\
            .then_inc(wq_loaded, 16)
        sp.dma_start(bq[:, :], b_qkv.partition_broadcast(P)).then_inc(tables_loaded, 16)
        sp.wait_ge(qk_ready, TOKEN_TILES)
        sp.wait_ge(raw_ready, 2 * TOKEN_TILES)
        sp.wait_ge(v_ready, TOKEN_TILES)
        sp.dma_start(wd[:, :, :], wdt.rearrange("(t p) n -> p t n", p=P)).then_inc(wd_loaded, 16)
        sp.dma_start(bd[:, :], b_d.partition_broadcast(P)).then_inc(wd_loaded, 16)

        def place_rowmax(g):
            sp.wait_ge(mrow_ready, num(g) + 1)
            for i in range(3):
                sp.dma_start(qa[buf(g)][ROWS + i:ROWS + i + 1, :, :], mrow[4 * i:4 * i + 4, :])\
                    .then_inc(m_placed, 16)

        with sp.Fori(0, GROUPS // BUF) as i:
            for u in range(BUF):
                place_rowmax((i, u))
        sp.wait_ge(pv_full, NU * GROUPS)
        sp.wait_ge(norm_ready, 2 * GROUPS)
        sp.wait_ge(spilled, 16)
        sp.dma_start(w13b_all[:, :], spill.ap()[:, 0:2 * W_T]).then_inc(w13_back, 16)
        sp.dma_start(w2b_all[:, :], spill.ap()[:, 2 * W_T:3 * W_T]).then_inc(w2_back, 16)
        for c in range(CHUNKS):
            sp.wait_ge(resid_ready, TOKEN_TILES + TPC * (c + 1))
            sp.dma_start(out_rows[:, TPC * c:TPC * (c + 1), :], x[:, TPC * c:TPC * (c + 1), :]).then_inc(out_stored, 16)
        sp.wait_ge(out_stored, 16 * CHUNKS)

    @block.gpsimd
    def _(pool):
        steps = [0]

        def chain(ins):
            steps[0] += 1
            ins.then_inc(pool_chain, 1)
            pool.wait_ge(pool_chain, steps[0])

        chain(nc.gpsimd.memset(ident[:, :], 0.0))
        chain(nc.gpsimd.memset(ident16[:, :], 0.0))
        chain(nc.gpsimd.memset(negmask[:, :], 0.0))
        for m in (ident, ident16):
            nc.gpsimd.affine_select(out=m[:, :], in_=m[:, :], compare_op=ALU.not_equal, fill=1.0, base=0,
                                    pattern=[[-1, P]], channel_multiplier=1).then_inc(consts_ready, 1)
        nc.gpsimd.affine_select(out=negmask[:, :], in_=negmask[:, :], compare_op=ALU.is_ge, fill=NEG, base=0,
                                pattern=[[-1, P]], channel_multiplier=1).then_inc(consts_ready, 1)

        def differences(w):
            _, slot, first, n, cols = WEIGHTS[w]
            for p in range(n):
                pool.wait_ge(w_loaded[first + p], 32)
                st = w_raw[:, w, p * cols:(p + 1) * cols]
                nc.gpsimd.tensor_tensor(out=st, in0=st, in1=wbase[slot][:, p * cols:(p + 1) * cols],
                                        op=ALU.subtract).then_inc(diff_ready, 1)

        def over_partitions(w):
            pool.wait_ge(part_ready, w + 1)
            nc.gpsimd.partition_all_reduce(allr[:, w, 0:1], part[:, w, 0:1], P, RADD).then_inc(allr_ready, 1)
            nc.gpsimd.partition_all_reduce(allr[:, w, 1:2], part[:, w, 1:2], P, RMAX).then_inc(allr_ready, 1)

        for w in range(3):
            differences(w)
            over_partitions(w)
        over_partitions(3)

        def wait(semaphore, value):
            pool.wait_ge(semaphore, value)
            if not isinstance(value, int):
                pool.sem_inc(pool_waited, 1)


        def split_steps(g):
            pair, odd = pair_of(g)
            rows = store[:, bass.ds(pair * SEQ_TILES, SEQ_TILES), :]
            q_in = rows[:, :, QW * odd:QW * (odd + 1)].rearrange("p t (h d) -> p t h d", d=HEAD)
            k_in = rows[:, :, 2 * QW + HEAD * odd:2 * QW + HEAD * (odd + 1)]
            q2, kk = parts_q[g[1] % 2], parts_k[g[1] % 2]
            qs = q2[:, :, :].rearrange("p (t h) r -> p t h r", h=Q_PER_KV)
            lq = left[:, :, 0:QW].rearrange("p t (h d) -> p t h d", d=HEAD)
            lk = left[:, :, QW:QW + HEAD]

            def slot(t, s):
                return t[:, :, HEAD * s:HEAD * (s + 1)]

            def slot4(s):
                return qs[:, :, :, HEAD * s:HEAD * (s + 1)]

            copy, sub = nc.gpsimd.tensor_copy, lambda o, a, b: nc.gpsimd.tensor_tensor(out=o, in0=a, in1=b, op=ALU.subtract)
            return [
                lambda: copy(slot4(0), q_in),
                lambda: copy(slot(kk, 0), k_in),
                lambda: sub(lq, q_in, slot4(0)),
                lambda: sub(lk, k_in, slot(kk, 0)),
                lambda: copy(slot4(1), lq),
                lambda: copy(slot(kk, 1), lk),
                lambda: sub(slot4(5), lq, slot4(1)),
                lambda: sub(slot(kk, 4), lk, slot(kk, 1)),
            ]

        def split(g, lo, hi):
            todo = split_steps(g)
            for n in range(lo, hi):
                if n == 0:
                    if not never(g, 2):
                        wait(qkt_full, 5 * (num(g) - 1))
                else:
                    wait(split_step, num(g) * NSPLIT + n)
                todo[n]().then_inc(split_step, 1)

        raw4 = [r[:, :, 0:QK].rearrange("p g (h d) -> p g h d", d=HEAD) for r in qkv_raw]
        c4, s4 = (t[:, :, :].rearrange("p g (h d) -> p g h d", d=HEAD) for t in (rot_c, rot_s))
        H2 = HEAD // 2
        pool.wait_ge(tables_loaded, 48)
        for i in range(TOKEN_TILES):
            r, tt = raw4[i % 2], i % SEQ_TILES
            pool.wait_ge(raw_ready, 2 * (i + 1))
            if i:
                pool.wait_ge(qk_ready, i)

            def table(t, lo, hi):
                return t[:, tt, lo:hi].unsqueeze(1).unsqueeze(1).to_broadcast([P, SEQ_PAIRS, QK // HEAD, hi - lo])

            if i < SEQ_TILES:
                nc.gpsimd.tensor_tensor(out=c4, in0=r, in1=table(cos, 0, HEAD), op=ALU.mult).then_inc(rot_ready, 1)
            for lo in (0, H2):
                nc.gpsimd.tensor_tensor(out=s4[:, :, :, lo:lo + H2], in0=r[:, :, :, H2 - lo:HEAD - lo],
                                        in1=table(sin, lo, lo + H2), op=ALU.mult).then_inc(rot_ready, 1)
            if i >= SEQ_TILES:
                if i == SEQ_TILES:
                    pool.wait_ge(qk_ready, SEQ_TILES)
                if i == EARLY:
                    pool.wait_ge(hlo_ready, CHUNKS * IT)
                n = NSPLIT // 4
                split((None, (i - SEQ_TILES) // 4), n * (i % 4), n * (i % 4 + 1))

        def copy_v(g):
            pair, odd = pair_of(g)
            if never(g, 1):
                wait(ones_ready, 2 * BUF)
            if not never(g, 3):
                wait(pv_full, NU * (num(g) - 2) + 1)
            nc.gpsimd.tensor_copy(vs[buf(g)][:, :, 0:HEAD], store[:, bass.ds(pair * SEQ_TILES, SEQ_TILES),
                                                                  QK + HEAD * odd:QK + HEAD * (odd + 1)])\
                .then_inc(vs_ready, 1)

        def mask_unit(g, u):
            d = DIAGONAL.index(u)
            wait(exp_ready, 2 * (num(g) * NU + u) + 2)
            p = probs[u % PBUF][:, :, 0:P]
            nc.gpsimd.affine_select(out=p, in_=p, compare_op=ALU.is_ge, fill=0.0, base=0,
                                    pattern=[[0, Q_PER_KV], [1, P]], channel_multiplier=-1).then_inc(diag_ready, 1)

        def body(k, first, second, ahead, tail):
            if first:
                copy_v(k)
            for s in range(NU):
                unit = unit_at(k, s, second, tail)
                if unit and unit[1] in DIAGONAL:
                    mask_unit(*unit)
                if ahead and s < NSPLIT:
                    split(shift(k, 2), s, s + 1)

        pool.wait_ge(qkv_full, TOKEN_TILES)
        pool.wait_ge(split_step, 2 * NSPLIT)
        for v in range(BUF):
            nc.gpsimd.memset(ka[v][ROWS:MROWS, :], 1.0).then_inc(ones_ready, 1)
            pool.wait_ge(ones_ready, 2 * v + 1)
            chain(nc.gpsimd.memset(vs[v][:, :, HEAD:32], 0.0))
            nc.gpsimd.memset(vs[v][:, :, HEAD:HEAD + 1], 1.0).then_inc(ones_ready, 1)
            pool.wait_ge(ones_ready, 2 * v + 2)
        pool.wait_ge(qk_ready, TOKEN_TILES)
        pool.wait_ge(v_ready, TOKEN_TILES)
        for k in (0, 1):
            body((None, k), True, k >= 1, True, False)
        with pool.Fori(0, 3) as i:
            for u in range(BUF):
                body((i, u + 2), True, True, True, True)
        for k in (14, 15, 16):
            body((None, k), k < GROUPS, True, False, True)

    @block.scalar
    def _(act):
        def signs(w, p):
            _, slot, first, n, cols = WEIGHTS[w]
            piece = first + p
            act.wait_ge(diff_ready, piece + 1)
            st = w_raw[:, w, p * cols:(p + 1) * cols]
            if p == 0 and w == 2:
                act.wait_ge(weff_ready, SLICES)
            nc.scalar.activation(wsign[slot][:, p * cols:(p + 1) * cols], st, ACT.Sign).then_inc(sign_ready, 1)
            nc.scalar.activation(st, st, ACT.Abs, accum_out=dabs[:, piece:piece + 1]).then_inc(sign_ready, 1)

        def split_hi(w, p):
            _, slot, first, n, cols = WEIGHTS[w]
            act.wait_ge(weff_ready, SLICES * w + p + 1)
            nc.scalar.activation(half(w, 0, p), slice_of(w, wbase[slot][:, :], p), ACT.Copy,
                                 scale=wc[:, w, 3:4]).then_inc(whi_ready, 1)

        def ln_hi(n, j):
            act.wait_ge(lnt_full, TPC * n + j + 1)
            nc.scalar.copy(xt_of(n)[0][:, :, j * P:(j + 1) * P],
                           ps[:, LNT + j % 2, :].rearrange("p (a b) -> p a b", a=HB)).then_inc(xhi_ready, 1)

        for p in range(4):
            signs(0, p)
            if p == 1:
                for j in range(TPC):
                    ln_hi(0, j)
        signs(1, 0)
        for p in range(SLICES):
            split_hi(0, p)
            if p in (1, 4):
                signs(1, 1 + p // 4)
        signs(1, 3)
        for p in range(SLICES):
            split_hi(1, p)
            if p >= 2:
                signs(2, p - 2)
        signs(2, 5)
        signs(2, 6)

        def silu(T, u, bufs):
            act.wait_ge(gate_full, T + 1)
            if not isinstance(T, int) or T >= 2:
                act.wait_ge(h_ready, T - 1)
            nc.scalar.activation(bufs["silu"][u][:, :], ps[:, GATE, :], ACT.Silu, scale=scal[:, 0:1])\
                .then_inc(silu_ready, 1)

        def h_hi(T, u, bufs):
            act.wait_ge(h_ready, T + 1)
            if not isinstance(T, int) or T >= 2:
                act.wait_ge(down_full, T - 1)
            nc.scalar.copy(bufs["hs"][u][0][:, :], bufs["h"][u][:, :]).then_inc(hhi_ready, 1)

        def ffn(f, bufs):
            for c in range(CHUNKS):
                T0 = f * CHUNKS * IT + c * IT
                ln = (1, 2, 3, 4)[c] if f == 0 else (9, 10, 11, None)[c]
                if f == 0 and c == 0:
                    act.wait_ge(dve_chain, SCAL_READY)
                for t in range(2 * FIRST[f, c]):
                    silu(T0 + t, t % 2, bufs)
                    h_hi(T0 + t, t % 2, bufs)
                    if f == 0 and c == 0:
                        for p in (2 * t, 2 * t + 1)[:SLICES - 2 * t]:
                            split_hi(2, p)
                if f == 0 and c == 2:
                    act.wait_ge(dve_chain, WQ_READY)
                    nc.scalar.activation(wq[0][:, :, :].rearrange("p a b -> p (a b)"), wq_raw[:, :], ACT.Copy,
                                         scale=wc[:, 3, 3:4]).then_inc(whi_ready, 1)
                with act.Fori(FIRST[f, c], 6) as i:
                    for t in (0, 1):
                        T = i * 2 + (T0 + t)
                        silu(T, t, bufs)
                        h_hi(T, t, bufs)
                for t in (IT - 2, IT - 1):
                    if t == IT - 2 and ln is not None:
                        ln_hi(ln, 0)
                        ln_hi(ln, 1)
                    silu(T0 + t, t % 2, bufs)
                    if t == IT - 2 and ln is not None:
                        ln_hi(ln, 2)
                        ln_hi(ln, 3)
                    h_hi(T0 + t, t % 2, bufs)

        ffn(0, ffn1)

        def take_qk(g, h):
            act.wait_ge(qkt_full, num(g) * 5 + h + 1)
            dst = ka[buf(g)][0:ROWS, :] if h == 4 else qa[buf(g)][0:ROWS, h, :]
            nc.scalar.copy(dst, ps[0:ROWS, SHARED_BANK, :].bitcast(BF16)).then_inc(qkt_act, 1)

        def repeat_parts(g):
            q2, kk = parts_q[g[1] % 2], parts_k[g[1] % 2]
            act.wait_ge(split_step, num(g) * NSPLIT + NSPLIT)
            nc.scalar.copy(q2[:, :, 2 * HEAD:4 * HEAD], q2[:, :, 0:2 * HEAD]).then_inc(dup_ready, 1)
            nc.scalar.copy(q2[:, :, 4 * HEAD:5 * HEAD], q2[:, :, 0:HEAD]).then_inc(dup_ready, 1)
            nc.scalar.copy(kk[:, :, 2 * HEAD:3 * HEAD], kk[:, :, HEAD:2 * HEAD]).then_inc(dup_ready, 1)
            nc.scalar.copy(kk[:, :, 3 * HEAD:6 * HEAD].rearrange("p t (s d) -> p t s d", d=HEAD)[:, :, 0:3:2, :],
                           kk[:, :, 0:HEAD].unsqueeze(2).to_broadcast([P, SEQ_TILES, 2, HEAD])).then_inc(dup_ready, 1)

        st4 = store[:, :, :].rearrange("p (g t) c -> p g t c", t=SEQ_TILES)
        for i in range(TOKEN_TILES):
            m, j = divmod(i, TPC)
            b, tt = divmod(i, SEQ_TILES)
            if m < CHUNKS - 1 and j == 2:
                ln_hi(5 + m, 0)
                ln_hi(5 + m, 1)
            if m < CHUNKS - 1 and j == 3:
                ln_hi(5 + m, 2)
                ln_hi(5 + m, 3)
            act.wait_ge(raw_ready, 2 * (i + 1))
            if i == 0:
                act.wait_ge(spilled, 16)
            nc.scalar.copy(st4[:, SEQ_PAIRS * b:SEQ_PAIRS * (b + 1), tt, QK:GW], qkv_raw[i % 2][:, :, QK:GW])\
                .then_inc(v_ready, 1)
            if i == EARLY:
                repeat_parts((None, 0))
            if i > EARLY:
                for h in range(2 * (i - EARLY) - 1, min(5, 2 * (i - EARLY) + 1)):
                    take_qk((None, 0), h)
        repeat_parts((None, 1))

        def exps(g, u):
            q0, q1, _ = unit_cols(u)
            U = num(g) * NU + u
            for pair in range(2):
                act.wait_ge(st_full, U * 2 + pair + 1)
                if not (never(g, 1) and u < PBUF):
                    act.wait_ge(pv_full, U - PBUF + 1)
                nc.scalar.activation(probs[u % PBUF][:, 2 * pair:2 * pair + 2, 0:q1 - q0],
                                     ps[:, 2 * pair:2 * pair + 2, 0:q1 - q0], ACT.Exp, scale=SM_SCALE)\
                    .then_inc(exp_ready, 1)

        def take_context(g, c):
            act.wait_ge(pv_full, num(g) * NU + (4 if c == 0 else NU))
            if c or not never(g, 1):
                act.wait_ge(ctxt_full, num(g) * 2 + c)
            nc.scalar.copy(ctx_sb[:, :], ps[:, CTX_BANK, :]).then_inc(ctx_ready, 1)

        def body(k, second, ahead, tail, further):
            for s in range(NU):
                unit = unit_at(k, s, second, tail)
                if unit:
                    exps(*unit)
                if s == TAILS and tail:
                    take_context(shift(k, -2), 1)
                use = SHARED.get(s)
                if use and use[0] == "qk" and use[1] in QK_ON_ACT and ahead:
                    take_qk(shift(k, 1), use[1])
                if s == TAILS + 4 and second:
                    take_context(shift(k, -1), 0)
                if s == REPEAT_AT and further:
                    repeat_parts(shift(k, 2))

        for k in (0, 1):
            body((None, k), k >= 1, True, False, True)
        with act.Fori(0, 3) as i:
            for u in range(BUF):
                body((i, u + 2), True, True, True, True)
        for k in (14, 15, 16, 17):
            body((None, k), k <= GROUPS, k + 1 < GROUPS, True, False)

        def take_ctx_t(i):
            act.wait_ge(dt_full, i + 1)
            if i >= 2:
                act.wait_ge(dense_full, i - 1)
            nc.scalar.copy(ctx_t[i % 2][:, :, :].rearrange("p a b -> p (a b)"), ps[:, 4 + i % 2, :])\
                .then_inc(ctx_t_ready, 1)

        for i in range(TOKEN_TILES):
            take_ctx_t(i)
            if i in (12, 13):
                ln_hi(8, 2 * (i - 12))
                ln_hi(8, 2 * (i - 12) + 1)
        ffn(1, ffn2)

    @block.vector
    def _(dve):
        steps = [0]

        def chain(ins):
            steps[0] += 1
            ins.then_inc(dve_chain, 1)
            dve.wait_ge(dve_chain, steps[0])

        def norm_stats(n):
            m = n % 4
            x_tiles_ready(dve, n)
            for j in range(TPC):
                nc.vector.bn_stats(out=stats[:, j, :], in_=x[:, TPC * m + j, :]).then_inc(dve_chain, 1)
            steps[0] += TPC
            dve.wait_ge(dve_chain, steps[0])
            for j in range(TPC):
                nc.vector.bn_aggr(out=mean_var[:, m, j, :], in_=stats[:, j, :]).then_inc(dve_chain, 1)
            steps[0] += TPC
            dve.wait_ge(dve_chain, steps[0])
            var, y, a, b = (nw[:, i, :] for i in range(4))
            chain(nc.vector.tensor_scalar(var, mean_var[:, m, :, 1], EPS, None, ALU.add))
            chain(nc.vector.tensor_scalar(a.bitcast(I32), var.bitcast(I32), 1, None, ALU.logical_shift_right))
            chain(nc.vector.tensor_scalar(y.bitcast(I32), a.bitcast(I32), -1, RSQRT_SEED, ALU.mult, ALU.add))
            for _ in range(3):
                chain(nc.vector.tensor_tensor(out=a, in0=y, in1=y, op=ALU.mult))
                chain(nc.vector.tensor_tensor(out=b, in0=a, in1=var, op=ALU.mult))
                chain(nc.vector.tensor_scalar(a, b, -0.5, 1.5, ALU.mult, ALU.add))
                chain(nc.vector.tensor_tensor(out=y, in0=y, in1=a, op=ALU.mult))
            chain(nc.vector.tensor_scalar(rstd[:, m, :], y, XS, None, ALU.mult))

        def normalised(n):
            m = n % 4
            if n:
                dve.wait_ge(lnt_full, TPC * n)
            for j in range(TPC):
                nc.vector.tensor_scalar(xnorm[j][:, :], x[:, TPC * m + j, :], mean_var[:, m, j, 0:1],
                                        rstd[:, m, j:j + 1], ALU.subtract, ALU.mult).then_inc(xnorm_ready, 1)

        def layer_norm(n):
            norm_stats(n)
            normalised(n)

        def ln_lo(n, j):
            dve.wait_ge(xhi_ready, TPC * n + j + 1)
            nc.vector.tensor_tensor(out=xt_of(n)[1][:, :, j * P:(j + 1) * P],
                                    in0=ps[:, LNT + j % 2, :].rearrange("p (a b) -> p a b", a=HB),
                                    in1=xt_of(n)[0][:, :, j * P:(j + 1) * P], op=ALU.subtract).then_inc(xlo_ready, 1)

        def base_max(w, p):
            _, slot, first, n, cols = WEIGHTS[w]
            dve.wait_ge(w_loaded[first + p], 32)
            nc.vector.tensor_reduce(bmax[:, first + p:first + p + 1], wbase[slot][:, p * cols:(p + 1) * cols],
                                    AX.X, ALU.max, apply_absolute_value=True).then_inc(bmax_ready, 1)

        def power_of_two(w):
            bound, e, s, inv = (wc[:, w, i:i + 1] for i in (1, 2, 3, 4))
            tmp = wc[:, w, 5:6]
            chain(nc.vector.tensor_scalar(bound, bound, 2.0 ** -30, None, ALU.max))
            chain(nc.vector.tensor_scalar(e.bitcast(I32), bound.bitcast(I32), 23, None, ALU.logical_shift_right))
            chain(nc.vector.tensor_scalar(tmp.bitcast(I32), e.bitcast(I32), -1, 268, ALU.mult, ALU.add))
            chain(nc.vector.tensor_scalar(s.bitcast(I32), tmp.bitcast(I32), 23, None, ALU.logical_shift_left))
            chain(nc.vector.tensor_scalar(tmp.bitcast(I32), e.bitcast(I32), -14, None, ALU.add))
            chain(nc.vector.tensor_scalar(inv.bitcast(I32), tmp.bitcast(I32), 23, None, ALU.logical_shift_left))

        def weight_stats(w):
            _, slot, first, n, cols = WEIGHTS[w]
            dve.wait_ge(sign_ready, 2 * (first + n))
            dve.wait_ge(bmax_ready, first + n)
            nc.vector.tensor_reduce(part[:, w, 0:1], dabs[:, first:first + n], AX.X, ALU.add)
            nc.vector.tensor_reduce(part[:, w, 1:2], bmax[:, first:first + n], AX.X, ALU.max).then_inc(part_ready, 1)
            dve.wait_ge(allr_ready, 2 * (w + 1))
            chain(nc.vector.tensor_scalar(wc[:, w, 0:1], allr[:, w, 0:1], 1.0 / (INTER * HID), None, ALU.mult))
            chain(nc.vector.tensor_tensor(out=wc[:, w, 1:2], in0=wc[:, w, 0:1], in1=allr[:, w, 1:2], op=ALU.add))
            power_of_two(w)

        def effective(w, p):
            _, slot, first, n, cols = WEIGHTS[w]
            b = slice_of(w, wbase[slot][:, :], p)
            nc.vector.scalar_tensor_tensor(out=b, in0=slice_of(w, wsign[slot][:, :], p), scalar=wc[:, w, 0:1],
                                           in1=b, op0=ALU.mult, op1=ALU.add).then_inc(weff_ready, 1)

        def split_lo(w, p):
            _, slot, first, n, cols = WEIGHTS[w]
            dve.wait_ge(whi_ready, SLICES * w + p + 1)
            nc.vector.scalar_tensor_tensor(out=half(w, 1, p), in0=slice_of(w, wbase[slot][:, :], p),
                                           scalar=wc[:, w, 3:4], in1=half(w, 0, p), op0=ALU.mult,
                                           op1=ALU.subtract).then_inc(wlo_ready, 1)

        def finish_weight(w):
            for p in range(SLICES + 1):
                if p < SLICES:
                    effective(w, p)
                if p:
                    split_lo(w, p - 1)

        layer_norm(0)
        for p in range(4):
            base_max(0, p)
        for j in range(TPC):
            ln_lo(0, j)
        base_max(1, 0)
        weight_stats(0)
        chain(nc.vector.tensor_scalar(scal[:, 0:1], wc[:, 0, 4:5], 1.0 / XS, None, ALU.mult))
        chain(nc.vector.tensor_scalar(scal[:, 1:2], wc[:, 0, 3:4], 1.0 / (XS * H_BOUND), None, ALU.mult))
        assert steps[0] == SCAL_READY, steps[0]
        finish_weight(0)
        for p in range(1, 4):
            base_max(1, p)
        weight_stats(1)
        finish_weight(1)
        for p in range(7):
            base_max(2, p)
        weight_stats(2)
        chain(nc.vector.tensor_scalar(scal[:, 4:5], wc[:, 0, 4:5], 0.5 * H_BOUND, wc[:, 1, 4:5], ALU.mult, ALU.mult))
        chain(nc.vector.tensor_tensor(out=scal[:, 2:3], in0=scal[:, 4:5], in1=wc[:, 2, 4:5], op=ALU.mult))

        def product(T, u, bufs):
            dve.wait_ge(up_full, T + 1)
            dve.wait_ge(silu_ready, T + 1)
            if not isinstance(T, int) or T >= 2:
                dve.wait_ge(hhi_ready, T - 1)
                dve.wait_ge(hlo_ready, T - 1)
            nc.vector.scalar_tensor_tensor(out=bufs["h"][u][:, :], in0=ps[:, UP, :], scalar=scal[:, 1:2],
                                           in1=bufs["silu"][u][:, :], op0=ALU.mult, op1=ALU.mult).then_inc(h_ready, 1)

        def h_lo(T, u, bufs):
            dve.wait_ge(hhi_ready, T + 1)
            dve.wait_ge(h_ready, T + 1)
            nc.vector.tensor_tensor(out=bufs["hs"][u][1][:, :], in0=bufs["h"][u][:, :], in1=bufs["hs"][u][0][:, :],
                                    op=ALU.subtract).then_inc(hlo_ready, 1)

        def residual(f, c):
            dve.wait_ge(down_full, f * CHUNKS * IT + (c + 1) * IT)
            if f == 1:
                dve.wait_ge(x2_ready, TPC * (c + 1))
            for j in range(TPC):
                xi = x[:, TPC * c + j, :]
                nc.vector.scalar_tensor_tensor(out=xi, in0=ps[:, DOWN + j, :], scalar=scal[:, 2:3], in1=xi,
                                               op0=ALU.mult, op1=ALU.add).then_inc(resid_ready, 1)

        def ffn(f, bufs):
            for c in range(CHUNKS):
                T0 = f * CHUNKS * IT + c * IT
                ln = (1, 2, 3, 4)[c] if f == 0 else (9, 10, 11, None)[c]
                for t in range(2 * FIRST[f, c]):
                    product(T0 + t, t % 2, bufs)
                    if f == 0 and c == 0:
                        effective(2, 2 * t)
                        if t:
                            split_lo(2, 2 * t - 1)
                    h_lo(T0 + t, t % 2, bufs)
                    if f == 0 and c == 0:
                        if t < 3:
                            effective(2, 2 * t + 1)
                        split_lo(2, 2 * t)
                    if c and t == 0:
                        residual(f, c - 1)
                if ln is not None:
                    layer_norm(ln)
                with dve.Fori(FIRST[f, c], 6) as i:
                    for t in (0, 1):
                        T = i * 2 + (T0 + t)
                        product(T, t, bufs)
                        h_lo(T, t, bufs)
                if f == 0 and c == 1:
                    dve.wait_ge(wq_loaded, 16)
                    nc.vector.tensor_reduce(part[:, 3, 1:2], wq_raw[:, :], AX.X, ALU.max, apply_absolute_value=True)
                    nc.vector.memset(part[:, 3, 0:1], 0.0).then_inc(part_ready, 1)
                    dve.wait_ge(allr_ready, 8)
                    chain(nc.vector.tensor_copy(wc[:, 3, 1:2], allr[:, 3, 1:2]))
                    power_of_two(3)
                    chain(nc.vector.tensor_scalar(scal[:, 3:4], wc[:, 3, 4:5], 1.0 / XS, None, ALU.mult))
                    assert steps[0] == WQ_READY, steps[0]
                if f == 0 and c == 2:
                    dve.wait_ge(whi_ready, 3 * SLICES + 1)
                    nc.vector.scalar_tensor_tensor(
                        out=wq[1][:, :, :].rearrange("p a b -> p (a b)"), in0=wq_raw[:, :], scalar=wc[:, 3, 3:4],
                        in1=wq[0][:, :, :].rearrange("p a b -> p (a b)"), op0=ALU.mult,
                        op1=ALU.subtract).then_inc(wlo_ready, 1)
                if (f, c) == (0, CHUNKS - 1):
                    norm_stats(5)
                for t in (IT - 2, IT - 1):
                    if t == IT - 2 and ln is not None:
                        for j in range(TPC):
                            ln_lo(ln, j)
                    product(T0 + t, t % 2, bufs)
                    h_lo(T0 + t, t % 2, bufs)
            residual(f, CHUNKS - 1)

        ffn(0, ffn1)

        dve.wait_ge(tables_loaded, 48)
        dve.wait_ge(spilled, 16)
        HALF = SEQ_PAIRS // 2

        def add_bias(i):
            b0 = 2 * (i % 2)
            dve.wait_ge(qkv_full, i + 1)
            if i >= 2:
                dve.wait_ge(v_ready, i - 1)
                dve.wait_ge(rot_ready, rotated(i - 2))
            for s in range(2):
                nc.vector.scalar_tensor_tensor(
                    out=qkv_raw[i % 2][:, HALF * s:HALF * (s + 1), :].rearrange("p a b -> p (a b)"),
                    in0=ps[:, b0 + s, 0:QKV // 2], scalar=scal[:, 3:4], in1=bq[:, s * QKV // 2:(s + 1) * QKV // 2],
                    op0=ALU.mult, op1=ALU.add).then_inc(raw_ready, 1)

        def take_qk(g, h):
            dve.wait_ge(qkt_full, num(g) * 5 + h + 1)
            nc.vector.tensor_copy(qa[buf(g)][0:ROWS, h, :], ps[0:ROWS, SHARED_BANK, :].bitcast(BF16)).then_inc(qkt_dve, 1)

        st4 = store[:, :, :].rearrange("p (g t) c -> p g t c", t=SEQ_TILES)

        def rotate(i):
            b, tt = divmod(i, SEQ_TILES)
            dve.wait_ge(rot_ready, rotated(i))
            nc.vector.tensor_tensor(out=st4[:, SEQ_PAIRS * b:SEQ_PAIRS * (b + 1), tt, 0:QK], in0=rot_c[:, :, :],
                                    in1=rot_s[:, :, :], op=ALU.add).then_inc(qk_ready, 1)

        for i in range(TOKEN_TILES):
            m, j = divmod(i, TPC)
            if m < CHUNKS - 1 and j == 1:
                normalised(5 + m)
            if m < CHUNKS - 1 and j == 2:
                ln_lo(5 + m, 0)
                ln_lo(5 + m, 1)
            if m < CHUNKS - 1 and j == 3:
                ln_lo(5 + m, 2)
                ln_lo(5 + m, 3)
            if i == EARLY + 1:
                take_qk((None, 0), 0)
            add_bias(i)
            if i:
                rotate(i - 1)
            if i >= SEQ_TILES:
                dve.wait_ge(raw_ready, 2 * (i + 1))
                dve.wait_ge(qk_ready, i)
                raw = qkv_raw[i % 2][:, :, 0:QK].rearrange("p g (h d) -> p g h d", d=HEAD)
                factor = cos[:, i % SEQ_TILES, :].unsqueeze(1).unsqueeze(1)
                chain(nc.vector.tensor_tensor(out=rot_c[:, :, :].rearrange("p g (h d) -> p g h d", d=HEAD), in0=raw,
                                              in1=factor.to_broadcast([P, SEQ_PAIRS, QK // HEAD, HEAD]), op=ALU.mult))
            if j == 3 and m < 2:
                norm_stats(6 + m)
        rotate(TOKEN_TILES - 1)

        def reduce_piece(k, r):
            qt, k0, w, heads = PIECES[r]
            dve.wait_ge(p1_full, num(k) * NP_ + r + 1)
            dst = rowmax[:, qt, heads[0]:heads[-1] + 1] if k0 == 0 else rowmax2[:, qt - 4, heads[0]:heads[-1] + 1]
            nc.vector.tensor_reduce(dst, ps[:, PASS1 + r % 2, 0:w * len(heads)].rearrange("p (h w) -> p h w", w=w),
                                    AX.X, ALU.max).then_inc(p1_read, 1)

        def split_rowmax(k):
            dve.wait_ge(p1_read, num(k) * NP_ + NP_)
            hi = rowmax[:, SEQ_TILES // 2:, :]
            nc.vector.tensor_tensor(out=hi, in0=hi, in1=rowmax2[:, :, :], op=ALU.max).then_inc(max_step, 1)
            dve.wait_ge(max_step, num(k) * 4 + 1)
            if not never(k, 1):
                dve.wait_ge(mt_full, num(k))
            nc.vector.tensor_scalar(nm[:, :, 0, :], rowmax[:, :, :], -1.0, None, ALU.mult).then_inc(max_step, 1)
            dve.wait_ge(max_step, num(k) * 4 + 2)
            nc.vector.scalar_tensor_tensor(out=rest[:, :, :], in0=rowmax[:, :, :], scalar=-1.0, in1=nm[:, :, 0, :],
                                           op0=ALU.mult, op1=ALU.subtract).then_inc(max_step, 1)
            dve.wait_ge(max_step, num(k) * 4 + 3)
            nc.vector.tensor_copy(nm[:, :, 1, :], rest[:, :, :]).then_inc(max_step, 1)
            dve.wait_ge(max_step, num(k) * 4 + 4)
            nc.vector.tensor_tensor(out=nm[:, :, 2, :], in0=rest[:, :, :], in1=nm[:, :, 1, :],
                                    op=ALU.subtract).then_inc(nm_ready, 1)

        def take_rowmax(g):
            dve.wait_ge(mt_full, num(g) + 1)
            if not never(g, 1):
                dve.wait_ge(m_placed, num(g) * 48)
            nc.vector.tensor_copy(mrow[:, :], ps[0:3 * Q_PER_KV, SHARED_BANK, :].bitcast(BF16)).then_inc(mrow_ready, 1)

        def normalise(g, c):
            pair, odd = pair_of(g)
            dve.wait_ge(ctxt_full, num(g) * 2 + c + 1)
            if c or not never(g, 1):
                dve.wait_ge(norm_ready, num(g) * 2 + c)
            t = ps[:, SHARED_BANK, :].rearrange("p (t h d) -> p t h d", t=4, h=Q_PER_KV)
            nc.vector.reciprocal(rec[:, :, :], t[:, :, :, HEAD]).then_inc(rec_ready, 1)
            dve.wait_ge(rec_ready, num(g) * 2 + c + 1)
            dst = store[:, bass.ds(pair * SEQ_TILES + 4 * c, 4), QW * odd:QW * (odd + 1)].rearrange("p t (h d) -> p t h d", d=HEAD)
            nc.vector.tensor_tensor(out=dst, in0=t[:, :, :, 0:HEAD],
                                    in1=rec[:, :, :].unsqueeze(3).to_broadcast([P, 4, Q_PER_KV, HEAD]),
                                    op=ALU.mult).then_inc(norm_ready, 1)

        def body(k, first, second, ahead, tail):
            for s in range(NU):
                if first:
                    for r in SLOTS[s]:
                        reduce_piece(k, r)
                use = SHARED.get(s)
                if use == ("rowmax", 0) and second:
                    take_rowmax(shift(k, -1))
                elif use == ("ctx", 1) and tail:
                    normalise(shift(k, -2), 1)
                elif use == ("ctx", 0) and second:
                    normalise(shift(k, -1), 0)
                elif use and use[0] == "qk" and use[1] in QK_ON_DVE and ahead:
                    take_qk(shift(k, 1), use[1])
            if first:
                split_rowmax(k)

        for k in (0, 1):
            body((None, k), True, k >= 1, True, False)
        with dve.Fori(0, 3) as i:
            for u in range(BUF):
                body((i, u + 2), True, True, True, True)
        for k in (14, 15, 16, 17):
            body((None, k), k < GROUPS, k <= GROUPS, k + 1 < GROUPS, True)

        dve.wait_ge(wd_loaded, 32)

        def bias_x(i):
            nc.vector.tensor_tensor(out=x[:, i, :], in0=x[:, i, :], in1=bd[:, :], op=ALU.add).then_inc(bias_ready, 1)

        bias_x(0)
        for i in range(TOKEN_TILES):
            if i + 1 < TOKEN_TILES:
                bias_x(i + 1)
            dve.wait_ge(dense_full, i + 1)
            dve.wait_ge(bias_ready, i + 1)
            nc.vector.tensor_tensor(out=x[:, i, :], in0=ps[:, i % 2, :], in1=x[:, i, :], op=ALU.add).then_inc(x2_ready, 1)
            if i == 8:
                layer_norm(8)
            if i in (12, 13):
                ln_lo(8, 2 * (i - 12))
                ln_lo(8, 2 * (i - 12) + 1)
        ffn(1, ffn2)

    @block.tensor
    def _(pe):
        mm, tr = nc.tensor.matmul, nc.tensor.transpose
        PASSES = ((0, 0), (0, 1), (1, 0))

        def ln_transpose(n, j):
            q = TPC * n + j
            pe.wait_ge(xnorm_ready, q + 1)
            if q >= 2:
                pe.wait_ge(xlo_ready, q - 1)
            for h in range(HB):
                last = tr(ps[:, LNT + j % 2, h * P:(h + 1) * P], xnorm[j][:, h * P:(h + 1) * P], ident[:, :])
            last.then_inc(lnt_full, 1)

        def up_product(bank, w, xt, t, full):
            for k in range(HB):
                for n, (a, b) in enumerate(PASSES):
                    last = mm(ps[:, bank, :], w[a][:, k, bass.ts(t, P)], xt[b][:, k, :],
                              start=(k == 0 and n == 0), stop=(k == HB - 1 and n == 2))
            last.then_inc(full, 1)

        def gate(T, t, w, xt):
            if not isinstance(T, int) or T:
                pe.wait_ge(silu_ready, T)
            up_product(GATE, w, xt, t, gate_full)

        def up(T, t, w, xt):
            if not isinstance(T, int) or T:
                pe.wait_ge(h_ready, T)
            up_product(UP, w, xt, t, up_full)

        def down(T, t, u, w, bufs, first, last_tile):
            pe.wait_ge(hhi_ready, T + 1)
            pe.wait_ge(hlo_ready, T + 1)
            hs = bufs["hs"][u]
            for j in range(TPC):
                for n, (a, b) in enumerate(PASSES):
                    last = mm(ps[:, DOWN + j, :], hs[a][:, j * P:(j + 1) * P], w[b][:, t, :],
                              start=(first and n == 0), stop=(last_tile and n == 2))
            last.then_inc(down_full, 1)

        def ffn(f, bufs, wa, wb, wc_):
            for c in range(CHUNKS):
                T0 = f * CHUNKS * IT + c * IT
                n = c + 8 * f
                xt = xt_of(n)
                ln = (1, 2, 3, 4)[c] if f == 0 else (9, 10, 11, None)[c]
                fresh = f == 0 and c == 0
                pe.wait_ge(xhi_ready, TPC * (n + 1))
                pe.wait_ge(xlo_ready, TPC * (n + 1))
                for t in range(2 * FIRST[f, c]):
                    if fresh:
                        pe.wait_ge(wlo_ready, t // 2 + 1)
                    gate(T0 + t, t, wa, xt)
                    if fresh:
                        pe.wait_ge(wlo_ready, SLICES + t // 2 + 1)
                    up(T0 + t, t, wb, xt)
                    if t:
                        if fresh:
                            pe.wait_ge(wlo_ready, 2 * SLICES + (t - 1) // 2 + 1)
                        if c and t == 1:
                            pe.wait_ge(resid_ready, TPC * (CHUNKS * f + c))
                        down(T0 + t - 1, t - 1, (t - 1) % 2, wc_, bufs, t == 1, False)
                    elif c:
                        down(T0 - 1, IT - 1, 1, wc_, bufs, False, True)
                with pe.Fori(FIRST[f, c], 6) as i:
                    for t in (0, 1):
                        T = i * 2 + (T0 + t)
                        gate(T, i * 2 + t, wa, xt)
                        up(T, i * 2 + t, wb, xt)
                        if fresh:
                            pe.wait_ge(wlo_ready, i + (2 * SLICES + t))
                        down(T - 1, i * 2 + (t - 1), 1 - t, wc_, bufs, False, False)
                for t in (IT - 2, IT - 1):
                    if t == IT - 2 and ln is not None:
                        ln_transpose(ln, 0)
                        ln_transpose(ln, 1)
                    gate(T0 + t, t, wa, xt)
                    if t == IT - 2 and ln is not None:
                        ln_transpose(ln, 2)
                        ln_transpose(ln, 3)
                    up(T0 + t, t, wb, xt)
                    down(T0 + t - 1, t - 1, (t - 1) % 2, wc_, bufs, False, False)
            down((f + 1) * CHUNKS * IT - 1, IT - 1, 1, wc_, bufs, False, True)

        pe.wait_ge(consts_ready, 3)
        for j in range(TPC):
            ln_transpose(0, j)
        ffn(0, ffn1, w1s, w3s, w2s)

        def transpose_qk(g, h):
            if h == 0:
                pe.wait_ge(dup_ready, num(g) * 4 + 4)
            bank = ps[0:ROWS, SHARED_BANK, :].bitcast(BF16)
            for tt in range(SEQ_TILES):
                src = parts_k[g[1] % 2][:, tt, :] if h == 4 else parts_q[g[1] % 2][:, Q_PER_KV * tt + h, :]
                last = tr(bank[:, tt * P:(tt + 1) * P], src, ident16[:, :])
            last.then_inc(qkt_full, 1)

        def first_operand(h):
            if h == 0:
                pe.wait_ge(xlo_ready, TPC * 8)
            elif h == 1:
                pe.wait_ge(qkt_dve, 1)
            else:
                pe.wait_ge(qkt_act, h - 1)
            transpose_qk((None, 0), h)

        def qkv(i):
            m, j = divmod(i, TPC)
            xt = xt_of(4 + m)
            if i == 0:
                pe.wait_ge(silu_ready, CHUNKS * IT)
                pe.wait_ge(h_ready, CHUNKS * IT)
                pe.wait_ge(whi_ready, 3 * SLICES + 1)
                pe.wait_ge(wlo_ready, 3 * SLICES + 1)
            if i == 1:
                pe.wait_ge(resid_ready, TOKEN_TILES)
            if i >= 2:
                pe.wait_ge(raw_ready, 2 * (i - 1))
            if j == 0:
                pe.wait_ge(xhi_ready, TPC * (5 + m))
                pe.wait_ge(xlo_ready, TPC * (5 + m))
            for s in range(2):
                for k in range(HB):
                    for n, (a, b) in enumerate(PASSES):
                        last = mm(ps[:, 2 * (i % 2) + s, 0:QKV // 2], xt[a][:, k, j * P:(j + 1) * P],
                                  wq[b][:, k, s * QKV // 2:(s + 1) * QKV // 2],
                                  start=(k == 0 and n == 0), stop=(k == HB - 1 and n == 2))
                if s == 0 and i > EARLY:
                    first_operand(2 * (i - EARLY - 1))
            last.then_inc(qkv_full, 1)
            if i in (EARLY + 1, EARLY + 2):
                first_operand(2 * (i - EARLY) - 1)

        for i in range(TOKEN_TILES):
            m, j = divmod(i, TPC)
            if m < CHUNKS - 1 and j == 2:
                ln_transpose(5 + m, 0)
                ln_transpose(5 + m, 1)
            if m < CHUNKS - 1 and j == 3:
                ln_transpose(5 + m, 2)
                ln_transpose(5 + m, 3)
            qkv(i)

        def shared_free(k, use, second, ahead, tail):
            happens = {("rowmax", 0): second, ("ctx", 1): tail, ("ctx", 0): second}
            before = [o for o in ORDER[:ORDER.index(use)] if happens.get(o, ahead)]
            n = num(k)
            if before:
                o = before[-1]
            elif never(k, GROUPS):
                o, n = ("qk", 4), num(k) - 1
            elif k[0] is None and k[1] >= GROUPS:
                o, n = ("ctx", 0), num(k) - 1
            else:
                o, n = ("qk", 4), n - 1
            if o == ("rowmax", 0):
                pe.wait_ge(mrow_ready, n)
            elif o == ("ctx", 1):
                pe.wait_ge(norm_ready, n * 2 - 2)
            elif o == ("ctx", 0):
                pe.wait_ge(norm_ready, n * 2 - 1)
            elif o[1] in QK_ON_DVE:
                pe.wait_ge(qkt_dve, n + 2)
            else:
                pe.wait_ge(qkt_act, n * 4 + 4 + o[1])

        def score_piece(k, r):
            qt, k0, w, heads = PIECES[r]
            v = buf(k)
            if r >= 2 or not never(k, 1):
                pe.wait_ge(p1_read, num(k) * NP_ + (r - 1))
            if r == 0:
                pe.wait_ge(qkt_act, num(k) * 4 + 4)
                pe.wait_ge(qkt_dve, num(k) + 1)
            diagonal = k0 + w == P * (qt + 1)
            for n, h in enumerate(heads):
                last = mm(ps[:, PASS1 + r % 2, n * w:(n + 1) * w], qa[v][0:ROWS, h, qt * P:(qt + 1) * P],
                          ka[v][0:ROWS, k0:k0 + w], start=True, stop=not diagonal)
                if diagonal:
                    last = mm(ps[:, PASS1 + r % 2, (n + 1) * w - P:(n + 1) * w], ident16[:, :], negmask[:, :],
                              start=False, stop=True)
            last.then_inc(p1_full, 1)

        def transpose_rowmax(g):
            pe.wait_ge(nm_ready, num(g) + 1)
            bank = ps[0:3 * Q_PER_KV, SHARED_BANK, :].bitcast(BF16)
            for qt in range(SEQ_TILES):
                last = tr(bank[:, qt * P:(qt + 1) * P], nm[:, qt, :, :].rearrange("p a b -> p (a b)"), ident16[:, :])
            last.then_inc(mt_full, 1)

        def scores_t(g, u, pair):
            q0, q1, _ = unit_cols(u)
            kt = UNITS[u][1]
            U, v = num(g) * NU + u, buf(g)
            if u == 0 and pair == 0:
                if never(g, 1):
                    pe.wait_ge(ones_ready, 2 * BUF)
                pe.wait_ge(m_placed, num(g) * 48 + 48)
            if u or not never(g, 1):
                pe.wait_ge(exp_ready, U * 2 + (pair - 1))
            for h in (2 * pair, 2 * pair + 1):
                last = mm(ps[:, h, 0:q1 - q0], ka[v][0:MROWS, kt * P:(kt + 1) * P], qa[v][0:MROWS, h, q0:q1],
                          start=True, stop=True)
            last.then_inc(st_full, 1)

        def values(g, u):
            c, kt = UNITS[u]
            q0, q1, at = unit_cols(u)
            v = buf(g)
            pe.wait_ge(exp_ready, (num(g) * NU + u) * 2 + 2)
            if u in DIAGONAL:
                pe.wait_ge(diag_ready, num(g) * ND + DIAGONAL.index(u) + 1)
            if u == 0:
                pe.wait_ge(vs_ready, num(g) + 1)
            first = u in (0, 4)
            if first and (c or not never(g, 1)):
                pe.wait_ge(ctx_ready, num(g) * 2 + c)
            for h in range(Q_PER_KV):
                last = mm(ps[32 * h:32 * h + 32, CTX_BANK, at:512], vs[v][:, kt, :], probs[u % PBUF][:, h, 0:q1 - q0],
                          start=first, stop=u in (3, NU - 1))
            last.then_inc(pv_full, 1)

        def transpose_context(g, c):
            pe.wait_ge(ctx_ready, num(g) * 2 + c + 1)
            for j in range(4):
                last = tr(ps[:, SHARED_BANK, j * P:(j + 1) * P], ctx_sb[:, j * P:(j + 1) * P], ident[:, :])
            last.then_inc(ctxt_full, 1)

        def body(k, first, second, ahead, tail):
            flags = second, ahead, tail
            for s in range(NU):
                todo = list(SLOTS[s]) if first else []
                unit, before = unit_at(k, s, second, tail), unit_before(k, s, second, tail)
                if s == TAILS:
                    for r in todo[:2]:
                        score_piece(k, r)
                    todo = todo[2:]
                if unit:
                    scores_t(*unit, 0)
                for r in todo[:1]:
                    score_piece(k, r)
                if unit:
                    scores_t(*unit, 1)
                for r in todo[1:2]:
                    score_piece(k, r)
                if before:
                    values(*before)
                for r in todo[2:]:
                    score_piece(k, r)
                use = SHARED.get(s)
                if use and use[0] == "qk" and ahead:
                    shared_free(k, use, *flags)
                    transpose_qk(shift(k, 1), use[1])
                elif use == ("rowmax", 0) and second:
                    shared_free(k, use, *flags)
                    transpose_rowmax(shift(k, -1))
                elif use == ("ctx", 1) and tail:
                    shared_free(k, use, *flags)
                    transpose_context(shift(k, -2), 1)
                elif use == ("ctx", 0) and second:
                    shared_free(k, use, *flags)
                    transpose_context(shift(k, -1), 0)

        pe.wait_ge(raw_ready, 2 * TOKEN_TILES)
        for k in (0, 1):
            body((None, k), True, k >= 1, True, False)
        with pe.Fori(0, 3) as i:
            for u in range(BUF):
                body((i, u + 2), True, True, True, True)
        for k in (14, 15, 16, 17):
            body((None, k), k < GROUPS, k <= GROUPS, k + 1 < GROUPS, True)

        st4 = store[:, :, :].rearrange("p (g t) c -> p g t c", t=SEQ_TILES)

        def transpose_rows(i):
            b, tt = divmod(i, SEQ_TILES)
            if i >= 2:
                pe.wait_ge(ctx_t_ready, i - 1)
            for q in range(HB):
                last = tr(ps[:, 4 + i % 2, q * P:(q + 1) * P], st4[:, SEQ_PAIRS * b + q, tt, 0:2 * QW], ident[:, :])
            last.then_inc(dt_full, 1)

        def project(i):
            pe.wait_ge(ctx_t_ready, i + 1)
            if i >= 2:
                pe.wait_ge(x2_ready, i - 1)
            for q in range(HB):
                last = mm(ps[:, i % 2, :], ctx_t[i % 2][:, q, :], wd[:, q, :], start=(q == 0), stop=(q == HB - 1))
            last.then_inc(dense_full, 1)

        pe.wait_ge(norm_ready, 2 * GROUPS)
        pe.wait_ge(wd_loaded, 32)
        pe.wait_ge(exp_ready, 2 * NU * GROUPS)
        pe.wait_ge(ctx_ready, 2 * GROUPS)
        transpose_rows(0)
        for i in range(TOKEN_TILES):
            if i + 1 < TOKEN_TILES:
                transpose_rows(i + 1)
            if i in (12, 13):
                ln_transpose(8, 2 * (i - 12))
                ln_transpose(8, 2 * (i - 12) + 1)
            project(i)
        pe.wait_ge(x2_ready, TOKEN_TILES)
        pe.wait_ge(w13_back, 16)
        pe.wait_ge(w2_back, 16)
        ffn(1, ffn2, w1b, w3b, w2b)

    ctx.close()


SLICES = IT // 2
FIRST = {(f, c): 2 if f == c == 0 else 1 for f in range(2) for c in range(CHUNKS)}
LN_STEPS = 4 + 4 + 3 + 12 + 1
WEIGHT_STEPS = 2 + 6
SCAL_READY = LN_STEPS + WEIGHT_STEPS + 2
WQ_READY = SCAL_READY + 2 * WEIGHT_STEPS + 2 + 2 * LN_STEPS + 1 + 6 + 1


def rotation_tables():
    inv = (1.0 / np.float32(1000000.0) ** (np.arange(0, HEAD, 2, dtype=np.float32) / np.float32(HEAD))).astype(np.float32)
    f = np.outer(np.arange(SEQ, dtype=np.float32), inv).astype(np.float32)
    c, s = np.cos(f).astype(np.float32), np.sin(f).astype(np.float32)
    return np.concatenate([c, c], 1), np.concatenate([-s, s], 1)


def kernel(**inputs):
    import concourse.bacc as bacc
    from concourse.bass_utils import run_bass_kernel_spmd

    def t(name):
        return np.ascontiguousarray(np.asarray(inputs[name]).T)

    def by_pair(a):
        a = a.reshape(a.shape[:-1] + (SEQ_PAIRS, 2, QKV // KV_HEADS))
        cut = [a[..., lo:hi].reshape(a.shape[:-2] + (-1,)) for lo, hi in ((0, QW), (QW, QW + HEAD), (QW + HEAD, QW + 2 * HEAD))]
        return np.ascontiguousarray(np.concatenate(cut, -1).reshape(a.shape[:-3] + (QKV,)))

    cos, sin = rotation_tables()
    arrays = {
        "x_in": np.ascontiguousarray(inputs["L0_attn_hidden_states"]).reshape(BATCH * SEQ, HID),
        "w1t": t("L0_ffn_w1"), "m1t": t("L0_ffn_mean_w1"), "w3t": t("L0_ffn_w3"), "m3t": t("L0_ffn_mean_w3"),
        "w2t": t("L0_ffn_w2"), "m2t": t("L0_ffn_mean_w2"), "wqkvt": by_pair(t("L0_attn_w_qkv")),
        "b_qkv": by_pair(np.asarray(inputs["L0_attn_b_qkv"])), "wdt": t("L0_attn_w_dense"),
        "b_d": np.ascontiguousarray(inputs["L0_attn_b_dense"]), "cos_in": cos, "sin_in": sin,
    }
    nc = bacc.Bacc("TRN2", target_bir_lowering=False, num_devices=1)
    args = [nc.dram_tensor(n, a.shape, mybir.dt.from_np(a.dtype), kind="ExternalInput").ap() for n, a in arrays.items()]
    args.append(nc.dram_tensor("y_out", (BATCH * SEQ, HID), F32, kind="ExternalOutput").ap())
    build(nc, *args)
    r = run_bass_kernel_spmd(nc, [arrays], core_ids=[0])
    return r.results[0]["y_out"].reshape(BATCH, SEQ, HID)
```
